# Optimizing a Trainium2 kernel written in Bass

```python
import numpy as np
import jax
import jax.numpy as jnp

def _softmax(x, axis=-1):
    return jax.nn.softmax(x, axis=axis)

def _gelu(x):
    return jax.nn.gelu(x, approximate=True)

def _silu(x):
    return jax.nn.silu(x)

def _sigmoid(x):
    return jax.nn.sigmoid(x)

def _layernorm(x, axis=-1, eps=1e-05):
    m = jnp.mean(x, axis=axis, keepdims=True)
    v = jnp.var(x, axis=axis, keepdims=True)
    return (x - m) / jnp.sqrt(v + eps)

def _scatter_add(tgt, idx, src, axis=0):
    return tgt.at[idx].add(src)

def _segment_sum(src, seg, n):
    return jax.ops.segment_sum(src, seg, n)
kernel_name = 'mk_gnn_resnorm_d2_gnn_r8_9817d6'

def setup_inputs(seed: int=0):
    np.random.seed(seed)
    _w = jnp.asarray

    def _rec_inputs():
        import jax
        import jax.numpy as jnp
        _gk = jax.random.key(seed)
        x = -0.0005121 + 1.001 * jax.random.normal(jax.random.fold_in(_gk, 1), (12500, 64), jnp.float32)
        src = jax.random.randint(jax.random.fold_in(_gk, 2), (400000,), 0, 12500, jnp.int32)
        dst = jnp.minimum((12500 * jax.random.uniform(jax.random.fold_in(_gk, 3), (400000,)) ** 2.0).astype(jnp.int32), 99999)
        _o = jnp.argsort(dst, stable=True)
        src = src[_o]
        dst = dst[_o]
        edge_weight = 0.000937891 + 0.999965 * jax.random.normal(jax.random.fold_in(_gk, 12), (400000,), jnp.float32)
        return (x, src, dst, edge_weight)
    x, src, dst, edge_weight = _rec_inputs()

    def _L0_gnn_setup():
        import jax, jax.numpy as jnp
        import numpy as np
        N, D, H, E = (6250, 64, 4, 100000)
        key = jax.random.key(seed)
        k1, k2, k3, k4, k5 = jax.random.split(key, 5)
        inputs = jax.random.normal(k1, (N, D), dtype=jnp.float32)
        Wh = jax.random.normal(k2, (H, D, D), dtype=jnp.float32) * (1.414 / np.sqrt(D))
        weight = jax.random.normal(k3, (H * D, D), dtype=jnp.float32) * (1.414 / np.sqrt(H * D))
        src = jax.random.randint(k4, (E,), 0, N, dtype=jnp.int64)
        dst = jax.random.randint(k5, (E,), 0, N, dtype=jnp.int64)
        return {'inputs': inputs, 'Wh': Wh, 'weight': weight, 'src': src, 'dst': dst}
    _L0_gnn_all = _L0_gnn_setup()
    _L0_gnn_in = {k: v for k, v in _L0_gnn_all.items() if k in ('Wh', 'weight')}
    del _L0_gnn_all

    def _L1_gnn_setup():
        import jax, jax.numpy as jnp
        import numpy as np
        N_NODES = 6250
        N_EDGES = 100000
        D = 64

        def _gnn_layer(nf, traj, src, dst, We, be, Wn, bn):
            ef = jnp.concatenate([nf[src], nf[dst], traj[:, None]], axis=-1)
            msg = jax.nn.leaky_relu(ef @ We.T + be, negative_slope=0.01)
            red = jax.ops.segment_sum(msg, dst, num_segments=nf.shape[0])
            h = jnp.concatenate([nf, red], axis=-1)
            return jax.nn.leaky_relu(h @ Wn.T + bn, negative_slope=0.01)
        key = jax.random.key(seed)
        ks = jax.random.split(key, 20)
        inp = {'nf': jax.random.normal(ks[0], (N_NODES, D), dtype=jnp.float32), 'traj': jax.random.normal(ks[1], (N_EDGES,), dtype=jnp.float32), 'src': jax.random.randint(ks[2], (N_EDGES,), 0, N_NODES), 'dst': jax.random.randint(ks[3], (N_EDGES,), 0, N_NODES)}
        s = 0.05
        for l in range(3):
            inp[f'We{l}'] = jax.random.normal(ks[4 + 4 * l], (D, 2 * D + 1), dtype=jnp.float32) * s
            inp[f'be{l}'] = jax.random.normal(ks[5 + 4 * l], (D,), dtype=jnp.float32) * s
            inp[f'Wn{l}'] = jax.random.normal(ks[6 + 4 * l], (D, 2 * D), dtype=jnp.float32) * s
            inp[f'bn{l}'] = jax.random.normal(ks[7 + 4 * l], (D,), dtype=jnp.float32) * s
        return inp
    _L1_gnn_all = _L1_gnn_setup()
    _L1_gnn_in = {k: v for k, v in _L1_gnn_all.items() if k in ('We0', 'be0', 'Wn0', 'bn0', 'We1', 'be1', 'Wn1', 'bn1', 'We2', 'be2', 'Wn2', 'bn2')}
    del _L1_gnn_all
    return {'x': x, 'src': src, 'dst': dst, 'edge_weight': edge_weight, 'L0_gnn_Wh': _L0_gnn_in['Wh'], 'L0_gnn_weight': _L0_gnn_in['weight'], 'L1_gnn_We0': _L1_gnn_in['We0'], 'L1_gnn_be0': _L1_gnn_in['be0'], 'L1_gnn_Wn0': _L1_gnn_in['Wn0'], 'L1_gnn_bn0': _L1_gnn_in['bn0'], 'L1_gnn_We1': _L1_gnn_in['We1'], 'L1_gnn_be1': _L1_gnn_in['be1'], 'L1_gnn_Wn1': _L1_gnn_in['Wn1'], 'L1_gnn_bn1': _L1_gnn_in['bn1'], 'L1_gnn_We2': _L1_gnn_in['We2'], 'L1_gnn_be2': _L1_gnn_in['be2'], 'L1_gnn_Wn2': _L1_gnn_in['Wn2'], 'L1_gnn_bn2': _L1_gnn_in['bn2']}

def reference(x, src, dst, edge_weight, L0_gnn_Wh, L0_gnn_weight, L1_gnn_We0, L1_gnn_be0, L1_gnn_Wn0, L1_gnn_bn0, L1_gnn_We1, L1_gnn_be1, L1_gnn_Wn1, L1_gnn_bn1, L1_gnn_We2, L1_gnn_be2, L1_gnn_Wn2, L1_gnn_bn2):
    import jax
    import jax.numpy as jnp

    def _L0_gnn_ref(inputs, Wh, weight, src, dst):
        import jax, jax.numpy as jnp
        import numpy as np
        N, D, H, E = (6250, 64, 4, 100000)
        n, d = inputs.shape
        h = inputs
        a = jnp.einsum('nd,hde->nhe', h, Wh)
        scores = jnp.sum(a * h[:, None, :], axis=-1) / jnp.sqrt(jnp.asarray(d, h.dtype))
        attn = jax.nn.softmax(scores, axis=0)
        msg = h[src][:, None, :] * attn[src][:, :, None]
        neigh = jax.ops.segment_sum(msg, dst, num_segments=n)
        out = neigh.reshape(n, -1) @ weight
        return jax.nn.elu(out)

    def _L1_gnn_ref(nf, traj, src, dst, We0, be0, Wn0, bn0, We1, be1, Wn1, bn1, We2, be2, Wn2, bn2):
        import jax, jax.numpy as jnp
        import numpy as np
        N_NODES = 6250
        N_EDGES = 100000
        D = 64

        def _gnn_layer(nf, traj, src, dst, We, be, Wn, bn):
            ef = jnp.concatenate([nf[src], nf[dst], traj[:, None]], axis=-1)
            msg = jax.nn.leaky_relu(ef @ We.T + be, negative_slope=0.01)
            red = jax.ops.segment_sum(msg, dst, num_segments=nf.shape[0])
            h = jnp.concatenate([nf, red], axis=-1)
            return jax.nn.leaky_relu(h @ Wn.T + bn, negative_slope=0.01)
        params = [(We0, be0, Wn0, bn0), (We1, be1, Wn1, bn1), (We2, be2, Wn2, bn2)]
        h = nf
        for We, be, Wn, bn in params:
            h = _gnn_layer(h, traj, src, dst, We, be, Wn, bn)
        return h
    x = _layernorm(x + _L0_gnn_ref(x, L0_gnn_Wh, L0_gnn_weight, src, dst), axis=-1)
    x = _layernorm(x + _L1_gnn_ref(x, edge_weight, src, dst, L1_gnn_We0, L1_gnn_be0, L1_gnn_Wn0, L1_gnn_bn0, L1_gnn_We1, L1_gnn_be1, L1_gnn_Wn1, L1_gnn_bn1, L1_gnn_We2, L1_gnn_be2, L1_gnn_Wn2, L1_gnn_bn2), axis=-1)
    return x

_drawn_inputs = setup_inputs


def setup_inputs(seed=0):
    import zlib

    import numpy as np

    out = dict(_drawn_inputs(seed))
    spreads = {}
    factors = {'edge_weight': 5.659,
     'L0_gnn_Wh': 8.0,
     'L0_gnn_weight': 8.0,
     'L1_gnn_bn0': 5.835,
     'L1_gnn_bn1': 8.0,
     'L1_gnn_be2': 5.194,
     'L1_gnn_bn2': 27.165}
    for name, (base, spread) in spreads.items():
        noise = np.random.default_rng([zlib.crc32(name.encode()), seed]).standard_normal(out[name].shape)
        drawn = base * np.exp(spread * noise) if base else spread * noise
        out[name] = jnp.asarray(drawn.astype(out[name].dtype))
    for name, factor in factors.items():
        out[name] = (out[name] * factor).astype(out[name].dtype)
    return out
```

```python
import numpy as np
import concourse.bass as bass
from concourse import mybir
from contextlib import ExitStack

F32, I32, BF16 = mybir.dt.float32, mybir.dt.int32, mybir.dt.bfloat16
ALU = mybir.AluOpType
ACT = mybir.ActivationFunctionType
AX = mybir.AxisListType

P = 128
N, D, H, E = 12500, 64, 4, 400000
LAYERS = 3
EPS = 1e-5
SLOPE = 0.01
NW = -(-N // P)
TAIL = N - (NW - 1) * P
ET = E // P
G = 8
BUF = 4
GROUPS = -(-(ET + NW - 1) // (G * BUF)) * BUF
LAPS = GROUPS // BUF
KB = -(-(GROUPS + BUF) * G // P)
PAIRS = KB * P
assert ET * P == E and G * D == 512


class Lane:

    def __init__(self, engine, sem):
        self.engine, self.sem, self.count = engine, sem, 0

    def did(self, instruction):
        self.count += 1
        instruction.then_inc(self.sem, 1)
        return self.sem, self.count

    def wait(self, *points):
        for sem, value in points:
            self.engine.wait_ge(sem, value)


def staged(count, stages):
    for t in range(count + len(stages) - 1):
        for s in reversed(range(len(stages))):
            if 0 <= t - s < count:
                stages[s](t - s)


def over(ap, axis, count):
    shape = list(ap.shape)
    shape.insert(axis, count)
    return ap.unsqueeze(axis).broadcast_to(shape)


def build(nc, x, src, dst, edge_weight, w_head, w_out, w_edge, b_edge, w_traj, w_node, b_node, out):
    ctx = ExitStack()

    def sb(name, shape, dt=F32):
        return ctx.enter_context(nc.sbuf_tensor(name, shape, dt))

    def sem(name):
        return ctx.enter_context(nc.semaphore(name))

    def dram(name, shape, dt):
        return nc.dram_tensor(name, shape, dt).ap()

    e_src, e_dst, e_wt = (dram(n, [ET, P], I32) for n in ("e_src", "e_dst", "e_wt"))
    tile_last = dram("tile_last", [1, ET], I32)
    pair_wt = dram("pair_wt", [PAIRS, P], I32)
    tables = [dram(f"table{n}", [NW * P, D], F32) for n in range(2)]

    hr = sb("hr", [P, NW, 2 * D])
    red1 = sb("red1", [P, NW, D])
    x1 = sb("x1", [P, NW, D])
    aux = sb("aux", [P, NW * 3 * D // 2])
    b_part = aux[:, :].bitcast(BF16).rearrange("p (w c) -> p w c", c=3 * D)
    pair_src = sb("pair_src", [P, PAIRS], I32)
    pair_dst = sb("pair_dst", [P, PAIRS], BF16)
    pair_win = sb("pair_win", [1, PAIRS], I32)
    ident = sb("ident", [P, P])
    ones = sb("ones", [P, P])
    lane_iota = sb("lane_iota", [P, P], BF16)
    whead = sb("whead", [D, H * D])
    wout = sb("wout", [D, H * D])
    wedge = sb("wedge", [D + 1, 2 * D])
    wnode = sb("wnode", [P, D])
    bnode = sb("bnode", [1, D])
    wtraj = sb("wtraj", [G, G * D])
    work = sb("work", [P, 7680])

    at = 0

    def cut(cols, dt=F32):
        nonlocal at
        ap = work[:, at:at + cols]
        at += cols
        return ap if dt is F32 else ap.bitcast(dt)

    gathered = [cut(G * D).rearrange("p (j d) -> p j d", d=D) for _ in range(BUF)]
    gather_idx = [cut(G, I32) for _ in range(BUF)]
    onehot = [cut(G * P).rearrange("p (j n) -> p j n", n=P) for _ in range(2)]
    onehot_t = [cut(G * P // 2, BF16) for _ in range(2)]
    zsum = [cut(G * D) for _ in range(1)]
    msg = [cut(G * D) for _ in range(2)]
    traj = [cut(P)[0:G, :] for _ in range(BUF)]
    assert at <= 7680, at

    bank = [ctx.enter_context(nc.psum_tensor(f"bank{n}", [P, 512], F32)) for n in range(8)]

    ve = Lane(nc.vector, sem("vector_steps"))
    ac = Lane(nc.scalar, sem("scalar_steps"))
    pe = Lane(nc.tensor, sem("tensor_steps"))
    po = Lane(nc.gpsimd, sem("pool_steps"))

    def dma(engine, dest, source, s, already=0):
        engine.dma_start(dest, source).then_inc(s, 16)
        return s, already + 16

    s_x, s_w = sem("s_x"), sem("s_w")
    tail_zero = ve.did(nc.vector.memset(hr[:, NW - 1, 0:D], 0.0))
    full = (NW - 1) * P
    nc.sync.dma_start(hr[:, 0:NW - 1, 0:D], x[0:full, :].rearrange("(w p) d -> p w d", p=P)).then_inc(s_x, 16)
    nc.sync.wait_ge(*tail_zero)
    nc.sync.dma_start(hr[0:TAIL, NW - 1, 0:D], x[full:N, :]).then_inc(s_x, 16)
    nc.scalar.dma_start(whead[:, :], w_head).then_inc(s_w, 16)
    nc.scalar.dma_start(wout[:, :], w_out).then_inc(s_w, 16)
    x_here, w_here = (s_x, 32), (s_w, 32)

    one = po.did(nc.gpsimd.memset(ones[:, :], 1.0))
    zero = po.did(nc.gpsimd.memset(ident[:, :], 0.0))
    upto = work[:, 7040:7168]
    neg_tail = work[:, 7168:7169]
    iota_i = work[:, 7170:7171].bitcast(I32)
    bound = work[:, 7172:7174]
    bound_i = work[:, 7174:7176].bitcast(I32)
    pair_of = work[:, 7176:7176 + KB]
    pair_of_i = work[:, 7204:7204 + KB].bitcast(I32)
    lane_i = work[:, 7240:7368].bitcast(I32)
    po.wait(one, zero)
    ident_ok = po.did(nc.gpsimd.affine_select(out=ident[:, :], in_=ident[:, :], compare_op=ALU.not_equal, fill=1.0,
                                              base=0, pattern=[[-1, P]], channel_multiplier=1))
    upto_ok = po.did(nc.gpsimd.affine_select(out=upto, in_=ones[:, :], compare_op=ALU.is_ge, fill=0.0,
                                             base=0, pattern=[[1, P]], channel_multiplier=-1))
    po.did(nc.gpsimd.memset(neg_tail, 0.0))
    po.wait((po.sem, po.count))
    po.did(nc.gpsimd.affine_select(out=neg_tail, in_=neg_tail, compare_op=ALU.is_ge, fill=-1e30,
                                   base=TAIL - 1, pattern=[[0, 1]], channel_multiplier=-1))
    po.did(nc.gpsimd.iota(bound_i, pattern=[[P, 2]], base=0, channel_multiplier=P))
    po.did(nc.gpsimd.iota(pair_of_i, pattern=[[P, KB]], base=0, channel_multiplier=1))
    consts = po.did(nc.gpsimd.iota(lane_i, pattern=[[1, P]], base=0, channel_multiplier=0))
    ve.wait(consts)
    ve.did(nc.vector.tensor_copy(bound, bound_i))
    ve.did(nc.vector.tensor_copy(pair_of, pair_of_i))
    vconst = ve.did(nc.vector.tensor_copy(lane_iota[:, :], lane_i))

    s_e = sem("s_edges")
    for dest, source in ((e_dst, dst), (e_src, src), (e_wt, edge_weight.bitcast(I32))):
        nc.scalar.dma_start(dest, source.rearrange("(t p) -> t p", p=P)).then_inc(s_e, 16)
    edges_here = (s_e, 48)

    last_i = aux[0:NW, 0:ET].bitcast(I32)
    below = aux[0:NW, ET:2 * ET]
    past = aux[0:NW, 0:PAIRS]
    win_base = aux[:, PAIRS:2 * PAIRS]
    edge_rows = [aux[:, 2 * PAIRS + n * 512:2 * PAIRS + (n + 1) * 512] for n in range(4)]
    small = work[:, 7370:7430]
    tile_of = work[:, 7440:7440 + KB].bitcast(I32)
    lo_hi_rows = work[0:NW, 6528:6784].bitcast(I32)
    lo_hi_below = work[0:NW, 6784:7040]
    pair_iota_i = x1[0:NW, 0:52, :].rearrange("p w d -> p (w d)")
    col = lambda n: small[0:NW, n:n + 1]
    full_tiles, first_idx = small[0:NW, 0:2], small[0:NW, 2:4]
    first_idx_i = small[0:NW, 4:6].bitcast(I32)
    inside = small[0:NW, 6:8]
    start = small[0:NW, 8:10]
    is_full, is_none = small[0:NW, 10:12], small[0:NW, 12:14]
    first_tile = small[0:NW, 14:16]
    last_tile, nonempty, pairs = col(16), col(17), col(18)
    one_delta = small[0:NW, 20:22]
    pairs_upto = col(22)
    pt = {}
    s_last, s_rows = sem("s_last"), sem("s_rows")

    def find_lasts():
        nc.sync.wait_ge(*edges_here)
        nc.sync.dma_start(aux[0:125, 0:25].bitcast(I32),
                          e_dst[:, P - 1:P].rearrange("(a b) o -> a (b o)", b=25),
                          allow_slow_non_contiguous=True).then_inc(s_last, 16)
        nc.sync.wait_ge(s_last, 16)
        nc.sync.dma_start(tile_last[0, :].rearrange("(a b) -> a b", b=25), aux[0:125, 0:25].bitcast(I32)).then_inc(s_last, 16)
        nc.sync.wait_ge(s_last, 32)
        nc.sync.dma_start(last_i, tile_last[0:1, :].broadcast_to([NW, ET])).then_inc(s_last, 16)

    def count_full():
        ve.wait((s_last, 48), vconst)
        for b in range(2):
            done = ve.did(nc.vector.tensor_scalar(below, last_i, bound[0:NW, b:b + 1], None, ALU.is_lt))
            ve.wait(done)
            done = ve.did(nc.vector.tensor_reduce(full_tiles[:, b:b + 1], below, AX.X, ALU.add))
            ve.wait(done)
        done = ve.did(nc.vector.tensor_scalar(first_idx, full_tiles, float(ET - 1), None, ALU.min))
        ve.wait(done)
        pt["idx"] = ve.did(nc.vector.tensor_copy(first_idx_i, first_idx))
        po.wait(pt["idx"])
        for b in range(2):
            nc.gpsimd.indirect_dma_start(lo_hi_rows[:, b * P:(b + 1) * P], None, e_dst,
                                         bass.IndirectOffsetOnAxis(ap=first_idx_i[:, b:b + 1], axis=0)).then_inc(s_rows, 16)

    def count_pairs():
        ve.wait((s_rows, 32))
        for b in range(2):
            done = ve.did(nc.vector.tensor_scalar(lo_hi_below[:, b * P:(b + 1) * P], lo_hi_rows[:, b * P:(b + 1) * P],
                                                  bound[0:NW, b:b + 1], None, ALU.is_lt))
        ve.wait(done)
        done = ve.did(nc.vector.tensor_reduce(inside, lo_hi_below.rearrange("p (b e) -> p b e", b=2), AX.X, ALU.add))
        ve.wait(done)
        ve.did(nc.vector.scalar_tensor_tensor(start, first_idx, float(P), inside, ALU.mult, ALU.add))
        ve.did(nc.vector.tensor_scalar(is_full, inside, float(P), None, ALU.is_equal))
        done = ve.did(nc.vector.tensor_scalar(is_none, inside, 0.0, None, ALU.is_equal))
        ve.wait(done)
        ve.did(nc.vector.tensor_tensor(first_tile, first_idx, is_full, ALU.add))
        ve.did(nc.vector.tensor_tensor(last_tile, first_idx[:, 1:2], is_none[:, 1:2], ALU.subtract))
        done = ve.did(nc.vector.tensor_tensor(nonempty, start[:, 1:2], start[:, 0:1], ALU.is_gt))
        ve.wait(done)
        done = ve.did(nc.vector.tensor_tensor(pairs, last_tile, first_tile[:, 0:1], ALU.subtract))
        ve.wait(done)
        done = ve.did(nc.vector.scalar_tensor_tensor(pairs, pairs, 1.0, nonempty, ALU.add, ALU.mult))
        ve.wait(done)
        done = ve.did(nc.vector.tensor_tensor(one_delta[:, 1:2], first_tile[:, 1:2], first_tile[:, 0:1], ALU.subtract))
        ve.wait(done)
        ve.did(nc.vector.memset(one_delta[:, 0:1], 1.0))
        pt["pairs"] = ve.did(nc.vector.tensor_tensor(one_delta[:, 1:2], one_delta[:, 1:2], pairs, ALU.subtract))

    def sum_pairs():
        pe.wait(pt["pairs"], upto_ok, pt["bank7"])
        done = pe.did(nc.tensor.matmul(bank[7][0:NW, 0:1], upto[0:NW, 0:NW], pairs, start=True, stop=True))
        ve.wait(done)
        done = ve.did(nc.vector.tensor_copy(pairs_upto, bank[7][0:NW, 0:1]))
        po.wait(pt["idx"])
        done_i = po.did(nc.gpsimd.iota(win_base[0:NW, :].bitcast(I32), pattern=[[1, PAIRS]], base=0, channel_multiplier=0))
        ve.wait(done, done_i)
        pt["past"] = ve.did(nc.vector.tensor_scalar(past, win_base[0:NW, :].bitcast(I32), pairs_upto, None, ALU.is_ge))

    def place_pairs():
        pe.wait(pt["past"], pt["bank7"])
        for b in range(KB):
            done = pe.did(nc.tensor.matmul(bank[7][:, 2 * b:2 * b + 2], past[:, b * P:(b + 1) * P], one_delta,
                                           start=True, stop=True))
        tiles = small[:, 30:30 + KB]
        ve.wait(done)
        done = ve.did(nc.vector.tensor_tensor(tiles, bank[7][:, 0:2 * KB].rearrange("p (b c) -> p b c", c=2)[:, :, 1],
                                              pair_of, ALU.add))
        ve.wait(done)
        pt["tiles"] = ve.did(nc.vector.tensor_scalar(tile_of, tiles, float(ET - 1), None, ALU.min))
        for c in range(-(-PAIRS // 512)):
            a, b = c * 512, min((c + 1) * 512, PAIRS)
            pe.wait(pt["tiles"] if c == 0 else done)
            summed = pe.did(nc.tensor.matmul(bank[7][:, 0:b - a], ones[0:NW, :], past[:, a:b], start=True, stop=True))
            ve.wait(summed)
            ve.did(nc.vector.tensor_scalar(win_base[:, a:b], bank[7][:, 0:b - a], float(P), None, ALU.mult))
            done = ve.did(nc.vector.tensor_scalar(pair_win[:, a:b], bank[7][0:1, 0:b - a], float(NW - 1), None, ALU.min))
        pt["win"] = pt["bank7"] = done

    s_er = [sem(f"s_edge_rows{n}") for n in range(4)]
    rows_read = [None] * 4
    uses = [0] * 4

    def edge_columns(c):
        batches = list(range(4 * c, min(4 * c + 4, KB)))
        width = P * len(batches)
        for which, table in ((0, e_dst), (1, e_src)):
            n = 2 * (c % 2) + which
            rows = edge_rows[n]
            po.wait(pt["tiles"])
            if rows_read[n]:
                po.wait(*rows_read[n])
            for j, b in enumerate(batches):
                nc.gpsimd.indirect_dma_start(rows[:, j * P:(j + 1) * P].bitcast(I32), None, table,
                                             bass.IndirectOffsetOnAxis(ap=tile_of[:, b:b + 1], axis=0)).then_inc(s_er[n], 16)
            uses[n] += 16 * len(batches)

    def turn_columns(c):
        batches = list(range(4 * c, min(4 * c + 4, KB)))
        width = P * len(batches)
        for which in (0, 1):
            n = 2 * (c % 2) + which
            rows = edge_rows[n][:, 0:width]
            ve.wait((s_er[n], turned[c][which]))
            as_float = ve.did(nc.vector.tensor_copy(rows, rows.bitcast(I32)))
            pe.wait(as_float, pt["bank7"])
            for j in range(len(batches)):
                done = pe.did(nc.tensor.transpose(bank[7][:, j * P:(j + 1) * P], rows[:, j * P:(j + 1) * P], ident[:, :]))
            rows_read[n] = [done]
            ve.wait(done, pt["win"])
            a = 4 * c * P
            if which == 0:
                pt["bank7"] = ve.did(nc.vector.tensor_tensor(pair_dst[:, a:a + width], bank[7][:, 0:width],
                                                             win_base[:, a:a + width], ALU.subtract))
            else:
                pt["bank7"] = ve.did(nc.vector.tensor_copy(pair_src[:, a:a + width], bank[7][:, 0:width]))

    turned = {}

    def columns_step(c):
        if c < -(-KB // 4):
            edge_columns(c)
            turned[c] = (uses[2 * (c % 2)], uses[2 * (c % 2) + 1])
        if c > 0:
            turn_columns(c - 1)

    scores = work[:, 0:NW * H].rearrange("p (w h) -> p w h", h=H)
    attn = work[:, 400:400 + NW * H].rearrange("p (w h) -> p w h", h=H)
    prod = [work[:, 800 + n * 512:1312 + n * 512] for n in range(2)]
    half = NW // 2

    def xt(w):
        home = x1 if w < half else red1
        return home[0:D, :, :].rearrange("p w d -> p (w d)")[:, (w % half) * P:(w % half + 1) * P]

    assert 2 * half == NW and half * P == NW * D
    chunk = [(w, w + 2) for w in range(0, NW, 2)]
    turned_x, copied_x, headed, mixed = {}, {}, {}, {}
    pt["bank7"] = ident_ok

    def turn_x(c):
        pe.wait(x_here, ident_ok, *([copied_x[c - 2]] if c >= 2 else []))
        for j, w in enumerate(range(*chunk[c])):
            turned_x[c] = pe.did(nc.tensor.transpose(bank[c % 2][0:D, j * P:(j + 1) * P], hr[:, w, 0:D], ident[:, :]))

    def copy_x(c):
        ac.wait(turned_x[c])
        for j, w in enumerate(range(*chunk[c])):
            copied_x[c] = ac.did(nc.scalar.copy(xt(w), bank[c % 2][0:D, j * P:(j + 1) * P]))

    def head_x(c):
        pe.wait(w_here, copied_x[c], *([mixed[c - 2]] if c >= 2 else []))
        for j, w in enumerate(range(*chunk[c])):
            headed[c] = pe.did(nc.tensor.matmul(bank[2 + c % 2][:, j * H * D:(j + 1) * H * D], xt(w), whead[:, :],
                                                start=True, stop=True))

    def score_x(c):
        a, b = chunk[c]
        ve.wait(headed[c])
        mixed[c] = ve.did(nc.vector.tensor_tensor(
            prod[c % 2].rearrange("p (w h d) -> p w h d", h=H, d=D),
            bank[2 + c % 2][:, :].rearrange("p (w h d) -> p w h d", h=H, d=D), over(hr[:, a:b, 0:D], 2, H), ALU.mult))
        ve.wait(mixed[c])
        return ve.did(nc.vector.tensor_reduce(scores[:, a:b, :], prod[c % 2].rearrange("p (w h d) -> p w h d", h=H, d=D),
                                              AX.X, ALU.add))

    steps = {2: find_lasts, 14: count_full, 19: count_pairs, 23: sum_pairs, 27: place_pairs}
    for n in range(-(-KB // 4) + 1):
        steps[33 + 2 * n] = lambda n=n: columns_step(n)
    last_score = {}

    def score_step(c):
        last_score[0] = score_x(c)
        if c in steps:
            steps[c]()

    staged(len(chunk), [turn_x, copy_x, head_x, score_step])

    ve.wait(last_score[0], consts)
    done = ve.did(nc.vector.tensor_scalar(scores[:, NW - 1, :], scores[:, NW - 1, :], neg_tail, None, ALU.add))
    ve.wait(done)
    top = work[:, 1824:1828]
    top_t, diag, neg_top = work[0:H, 1830:1831], work[0:H, 1832:1836], work[:, 1836:1840]
    total, inverse = work[:, 1840:1844], work[:, 1844:1848]
    done = ve.did(nc.vector.tensor_reduce(top, scores.rearrange("p w h -> p h w"), AX.X, ALU.max))
    pe.wait(done)
    done = pe.did(nc.tensor.transpose(bank[0][0:H, 0:P], top, ident[:, :]))
    ve.wait(done)
    done = ve.did(nc.vector.tensor_reduce(top_t, bank[0][0:H, 0:P], AX.X, ALU.max))
    ve.wait(done)
    done = ve.did(nc.vector.tensor_scalar(diag, ident[0:H, 0:H], top_t, None, ALU.mult))
    pe.wait(done)
    done = pe.did(nc.tensor.matmul(bank[1][:, 0:H], ones[0:H, :], diag, start=True, stop=True))
    ve.wait(done)
    scale = float(D) ** -0.5
    done = ve.did(nc.vector.tensor_scalar(neg_top, bank[1][:, 0:H], -scale, None, ALU.mult))
    ac.wait(done)
    for h in range(H):
        done = ac.did(nc.scalar.activation(attn[:, :, h], scores[:, :, h], ACT.Exp, bias=neg_top[:, h:h + 1], scale=scale))
    ve.wait(done)
    done = ve.did(nc.vector.tensor_reduce(total, attn.rearrange("p w h -> p h w"), AX.X, ALU.add))
    pe.wait(done)
    done = pe.did(nc.tensor.matmul(bank[0][:, 0:H], ones[:, :], total, start=True, stop=True))
    ve.wait(done)
    done = ve.did(nc.vector.reciprocal(inverse, bank[0][:, 0:H]))
    ve.wait(done)
    attn_ok = ve.did(nc.vector.tensor_tensor(attn, attn, over(inverse, 1, NW), ALU.mult))

    ROWS = 14
    y_out = [work[:, 1856 + n * ROWS * D:1856 + (n + 1) * ROWS * D].rearrange("p (w d) -> p w d", d=D) for n in range(2)]
    s_t = [sem(f"s_table{n}") for n in range(2)]
    stores = [0, 0]
    weighted, summed_y = {}, {}

    def store(table, n, rows, source, point):
        nc.sync.wait_ge(*point)
        nc.sync.dma_start(table[rows[0] * P:rows[1] * P, :].rearrange("(w p) d -> p w d", p=P), source).then_inc(s_t[n], 16)
        stores[n] += 16
        return s_t[n], stores[n]

    y_stored = {}

    def out_x(c):
        pe.wait(attn_ok, *([weighted[c - 2]] if c >= 2 else []))
        for j, w in enumerate(range(*chunk[c])):
            headed[c] = pe.did(nc.tensor.matmul(bank[2 + c % 2][:, j * H * D:(j + 1) * H * D], xt(w), wout[:, :],
                                                start=True, stop=True))

    def sum_y(c):
        a, b = chunk[c]
        n, part = (a // ROWS) % 2, a // ROWS
        ve.wait(headed[c], attn_ok)
        weighted[c] = ve.did(nc.vector.tensor_tensor(
            prod[c % 2].rearrange("p (w h d) -> p w h d", h=H, d=D),
            bank[2 + c % 2][:, :].rearrange("p (w h d) -> p w h d", h=H, d=D), over(attn[:, a:b, :], 3, D), ALU.mult))
        ve.wait(weighted[c])
        if part >= 2 and a % ROWS == 0:
            ve.wait(y_stored[part - 2])
        done = ve.did(nc.vector.tensor_reduce(y_out[n][:, a % ROWS:a % ROWS + b - a, :],
                                              prod[c % 2].rearrange("p (w h d) -> p w d h", h=H, d=D), AX.X, ALU.add))
        if b % ROWS == 0:
            y_stored[part] = store(tables[0], n, (part * ROWS, (part + 1) * ROWS), y_out[n], done)

    staged(len(chunk), [out_x, sum_y])
    table_here = [(s_t[0], stores[0]), (s_t[1], stores[1])]

    s_pw, s_pr = sem("s_pair_weight"), sem("s_pair_rows")
    wt_rows = aux[:, 0:PAIRS]
    po.wait(pt["win"], pt["bank7"])
    for b in range(KB):
        nc.gpsimd.indirect_dma_start(wt_rows[:, b * P:(b + 1) * P].bitcast(I32), None, e_wt,
                                     bass.IndirectOffsetOnAxis(ap=tile_of[:, b:b + 1], axis=0)).then_inc(s_pr, 16)
    nc.sync.wait_ge(s_pr, 16 * KB)
    nc.sync.dma_start(pair_wt.rearrange("(b p) e -> p b e", p=P),
                      wt_rows.bitcast(I32).rearrange("p (b e) -> p b e", e=P)).then_inc(s_pw, 16)
    pair_wt_f = pair_wt.bitcast(F32)

    def edge_pass(number, table, table_points, layered):
        name = f"pass{number}_"
        s_idx, s_oh, s_zs, s_msg, s_acc, s_sc, s_tr, s_ot, s_z = (
            sem(name + n) for n in ("idx", "onehot", "zsum", "msg", "add", "scatter", "turn", "onehot_t", "z"))
        s_go = sem(name + "go")
        s_g = [sem(f"{name}gather{n}") for n in range(BUF)]
        s_tj = [sem(f"{name}traj{n}") for n in range(BUF)]
        turned_ps = [bank[n][:, :].bitcast(BF16) for n in range(2)]
        turned_f = [[bank[n], bank[2 + n]] for n in range(2)]
        z_ps = [bank[4], bank[5]]
        sum_ps = [bank[6], bank[7]]
        for e in (nc.vector, nc.gpsimd, nc.tensor, nc.scalar, nc.sync):
            for point in table_points:
                e.wait_ge(*point)
        block = nc.Block()
        block.__enter__()

        @block.gpsimd
        def _(pool):
            with pool.Fori(0, LAPS) as i:
                for q in range(BUF):
                    pool.wait_ge(s_idx, i * BUF + q + 1)
                    pool.sem_inc(s_go)
                    for j in range(G):
                        pool.indirect_dma_start(gathered[q][:, j, :], None, table,
                                                bass.IndirectOffsetOnAxis(ap=gather_idx[q][:, j:j + 1], axis=0)
                                                ).then_inc(s_g[q], 16)

        @block.vector
        def _(vec):
            def copy_idx(g0, q):
                vec.tensor_copy(gather_idx[q], pair_src[:, bass.ds(g0 * G, G)]).then_inc(s_idx, 1)

            def make_onehot(g0, n):
                rel = pair_dst[:, bass.ds(g0 * G, G)]
                vec.tensor_tensor(onehot[n], over(lane_iota[:, :], 1, G), over(rel, 2, P), ALU.is_equal).then_inc(s_oh, 1)

            vec.memset(hr[:, :, D:2 * D], 0.0).then_inc(s_acc, 1)
            vec.memset(red1[:, :, :], 0.0).then_inc(s_acc, 1)
            for g in range(BUF - 1):
                copy_idx(g, g)
            make_onehot(0, 0)
            with vec.Fori(0, LAPS) as i:
                for q in range(BUF):
                    g = i * BUF + q
                    copy_idx(g + (BUF - 1), (q + BUF - 1) % BUF)
                    make_onehot(g + 1, (q + 1) % 2)
                    if layered:
                        vec.wait_ge(s_z, g + 1)
                        vec.wait_ge(s_g[q], (i + 1) * (16 * G))
                        vec.tensor_tensor(zsum[0], z_ps[q % 2][:, :], gathered[q].rearrange("p j d -> p (j d)"),
                                          ALU.add).then_inc(s_zs, 1)
                        vec.wait_ge(s_zs, g + 1)
                        vec.scalar_tensor_tensor(msg[q % 2], zsum[0], SLOPE, zsum[0], ALU.mult, ALU.max).then_inc(s_msg, 1)
                    regs = [vec.alloc_register(f"{name}win{q}_{j}") for j in range(G)]
                    vec.load(regs, pair_win[0:1, bass.ds(g * G, G)])
                    vec.wait_ge(s_sc, g + 1)
                    for j in range(G):
                        w = vec.snap(regs[j], donate=True, min_val=0, max_val=NW - 1)
                        vec.wait_ge(s_acc, g * G + j + 1)
                        home = hr[:, bass.ds(w, 1), D:2 * D] if j % 2 == 0 else red1[:, bass.ds(w, 1), :]
                        vec.tensor_tensor(home, home, sum_ps[q % 2][:, j * D:(j + 1) * D].unsqueeze(1),
                                          ALU.add).then_inc(s_acc, 1)

        @block.tensor
        def _(ten):
            def turn_onehot(q):
                for j in range(G):
                    last = ten.transpose(turned_f[q % 2][j // 4][:, (j % 4) * P:(j % 4 + 1) * P], onehot[q % 2][:, j, :],
                                         ident[:, :])
                last.then_inc(s_tr, 1)

            def pre_message(g0, q):
                regs = [ten.alloc_register(f"{name}pwin{q}_{j}") for j in range(G)]
                ten.load(regs, pair_win[0:1, bass.ds(g0 * G, G)])
                ten.matmul(z_ps[q % 2][:, :], traj[q % BUF], wtraj[:, :], start=True, stop=False, skip_group_check=True)
                for j in range(G):
                    w = ten.snap(regs[j], donate=True, min_val=0, max_val=NW - 1)
                    for part in range(3):
                        last = ten.matmul(z_ps[q % 2][:, j * D:(j + 1) * D], onehot_t[q % 2][:, j * P:(j + 1) * P],
                                          b_part[:, bass.ds(w, 1), part * D:(part + 1) * D], start=False,
                                          stop=part == 2, skip_group_check=True)
                last.then_inc(s_z, 1)

            if layered:
                ten.wait_ge(s_oh, 1)
                turn_onehot(0)
                ten.wait_ge(s_ot, 1)
                ten.wait_ge(s_tj[0], 16)
                pre_message(0, 0)
            with ten.Fori(0, LAPS) as i:
                for q in range(BUF):
                    g = i * BUF + q
                    if layered:
                        ten.wait_ge(s_oh, g + 2)
                        turn_onehot(q + 1)
                        ten.wait_ge(s_msg, g + 1)
                    else:
                        ten.wait_ge(s_oh, g + 1)
                        ten.wait_ge(s_g[q], (i + 1) * (16 * G))
                        ten.wait_ge(s_acc, g * G + 2)
                    for j in range(G):
                        rows = msg[q % 2][:, j * D:(j + 1) * D] if layered else gathered[q][:, j, :]
                        last = ten.matmul(sum_ps[q % 2][:, j * D:(j + 1) * D], onehot[q % 2][:, j, :], rows,
                                          start=True, stop=True)
                    last.then_inc(s_sc, 1)
                    if layered:
                        ten.wait_ge(s_ot, g + 2)
                        ten.wait_ge(s_tj[(q + 1) % BUF], (i + (2 if q == BUF - 1 else 1)) * 16)
                        pre_message(g + 1, q + 1)

        if layered:
            @block.scalar
            def _(sca):
                def copy_turned(q):
                    for k in range(2):
                        last = sca.copy(onehot_t[q % 2][:, k * 512:(k + 1) * 512], turned_f[q % 2][k][:, :])
                    last.then_inc(s_ot, 1)

                sca.wait_ge(s_tr, 1)
                copy_turned(0)
                with sca.Fori(0, LAPS) as i:
                    for q in range(BUF):
                        sca.wait_ge(s_tr, i * BUF + q + 2)
                        copy_turned(q + 1)

            @block.sync
            def _(syn):
                def load_traj(g0, q):
                    syn.dma_start(traj[q], pair_wt_f[bass.ds(g0 * G, G), :]).then_inc(s_tj[q], 16)

                for q in range(BUF):
                    load_traj(q, q)
                with syn.Fori(0, LAPS) as i:
                    for q in range(BUF):
                        syn.wait_ge(s_z, i * BUF + q + 1)
                        load_traj(i * BUF + q + BUF, q)
                for q in range(BUF):
                    syn.wait_ge(s_tj[q], 16 * (LAPS + 1))

        block.__exit__(None, None, None)
        for e in (nc.vector, nc.scalar, nc.tensor, nc.sync, nc.gpsimd):
            e.wait_ge(s_acc, GROUPS * G + 2)
            e.wait_ge(s_oh, GROUPS + 1)
            if layered:
                e.wait_ge(s_z, GROUPS + 1)

    def normalise(value, count, dest, scratch, tmp):
        mean, var = scratch[:, 0:count], scratch[:, count:2 * count]
        ve.did(nc.vector.tensor_reduce(mean, value, AX.X, ALU.add))
        ve.wait((ve.sem, ve.count))
        ve.did(nc.vector.tensor_scalar(mean, mean, 1.0 / D, None, ALU.mult))
        ve.wait((ve.sem, ve.count))
        done = ve.did(nc.vector.tensor_tensor(value, value, over(mean, 2, D), ALU.subtract))
        ac.wait(done)
        done = ac.did(nc.scalar.activation(tmp, value, ACT.Square))
        ve.wait(done)
        done = ve.did(nc.vector.tensor_reduce(var, tmp, AX.X, ALU.add))
        ve.wait(done)
        done = ve.did(nc.vector.tensor_scalar(var, var, 1.0 / D, EPS, ALU.mult, ALU.add))
        ac.wait(done)
        done = ac.did(nc.scalar.activation(var, var, ACT.Sqrt))
        ve.wait(done)
        done = ve.did(nc.vector.reciprocal(var, var))
        ve.wait(done)
        return ve.did(nc.vector.tensor_tensor(dest, value, over(var, 2, D), ALU.mult))

    def attention_out(c):
        a, b = c * ROWS, (c + 1) * ROWS
        value = work[:, 0:ROWS * D].rearrange("p (w d) -> p w d", d=D)
        tmp = work[:, 1024:1024 + ROWS * D].rearrange("p (w d) -> p w d", d=D)
        scratch = work[:, 2048:2048 + 2 * ROWS]
        sums = hr[:, a:b, D:2 * D]
        done = ve.did(nc.vector.tensor_tensor(sums, sums, red1[:, a:b, :], ALU.add))
        ve.wait(done)
        done = ve.did(nc.vector.tensor_scalar(tmp, sums, 0.0, None, ALU.min))
        ac.wait(done)
        done = ac.did(nc.scalar.activation(tmp, tmp, ACT.Exp))
        done_v = ve.did(nc.vector.scalar_tensor_tensor(value, sums, 0.0, hr[:, a:b, 0:D], ALU.max, ALU.add))
        ve.wait(done, done_v)
        done = ve.did(nc.vector.scalar_tensor_tensor(value, tmp, -1.0, value, ALU.add, ALU.add))
        ve.wait(done)
        done = normalise(value, ROWS, x1[:, a:b, :], scratch, tmp)
        ve.wait(done)
        return ve.did(nc.vector.tensor_copy(hr[:, a:b, 0:D], x1[:, a:b, :]))

    QUAD = 4
    quads = [(w, min(w + QUAD, NW)) for w in range(0, NW, QUAD)]
    s_lw = sem("s_layer_weights")
    lw = [0]

    def load_layer(layer, engine_points):
        nc.sync.dma_start(wedge[0:D, :], w_edge[layer]).then_inc(s_lw, 16)
        nc.sync.dma_start(wedge[D:D + 1, :], b_edge[layer]).then_inc(s_lw, 16)
        for j in range(G):
            nc.sync.dma_start(wtraj[j:j + 1, j * D:(j + 1) * D], w_traj[layer]).then_inc(s_lw, 16)
        lw[0] += 16 * (2 + G)
        return s_lw, lw[0]

    def load_node(layer):
        nc.sync.dma_start(wnode[:, :], w_node[layer]).then_inc(s_lw, 16)
        nc.sync.dma_start(bnode[:, :], b_node[layer]).then_inc(s_lw, 16)
        lw[0] += 32
        return s_lw, lw[0]

    cat = [work[:, n * 512:(n + 1) * 512] for n in range(2)]
    feat = [work[0:D + 1, 1024 + n * 512:1024 + (n + 1) * 512] for n in range(2)]
    rest = [work[:, 2048 + n * 256:2048 + (n + 1) * 256].rearrange("p (w d) -> p w d", d=D) for n in range(2)]
    rest2 = [work[:, 2560 + n * 256:2560 + (n + 1) * 256].rearrange("p (w d) -> p w d", d=D) for n in range(2)]
    a_out = [work[:, 3072 + n * 256:3072 + (n + 1) * 256].rearrange("p (w d) -> p w d", d=D) for n in range(4)]

    def dense(node_here, edge_here, h_ready, table):
        t1, c1, u1, h1, t2, c2, ab, cp, b1, r1, b2, b3, st = ({} for _ in range(13))
        if edge_here:
            for f in feat:
                ones_row = ve.did(nc.vector.memset(f[D:D + 1, :], 1.0))

        def turn_both(q):
            pe.wait(h_ready(q), *([c1[q - 2]] if q >= 2 else []))
            for j, w in enumerate(range(*quads[q])):
                t1[q] = pe.did(nc.tensor.transpose(bank[q % 2][:, j * P:(j + 1) * P], hr[:, w, :], ident[:, :]))

        def copy_both(q):
            n = (quads[q][1] - quads[q][0]) * P
            ac.wait(t1[q], *([u1[q - 2]] if q >= 2 else []))
            c1[q] = ac.did(nc.scalar.copy(cat[q % 2][:, 0:n], bank[q % 2][:, 0:n]))

        def update(q):
            pe.wait(c1[q], node_here, *([h1[q - 2]] if q >= 2 else []))
            for j in range(quads[q][1] - quads[q][0]):
                o = bank[2 + q % 2][:, j * D:(j + 1) * D]
                pe.did(nc.tensor.matmul(o, ones[0:1, :], bnode[:, :], start=True, stop=False))
                u1[q] = pe.did(nc.tensor.matmul(o, cat[q % 2][:, j * P:(j + 1) * P], wnode[:, :], start=False, stop=True))

        def activate(q):
            a, b = quads[q]
            ve.wait(u1[q], *([y1[q - 2]] if q >= 2 else []))
            o = bank[2 + q % 2][:, 0:(b - a) * D].rearrange("p (w d) -> p w d", d=D)
            lin = rest[q % 2][:, 0:b - a, :] if not edge_here else hsave[q % 2][:, 0:b - a, :]
            y1[q] = ac_copy(q, lin, o)
            ve.wait(y1[q])
            h1[q] = ve.did(nc.vector.scalar_tensor_tensor(hr[:, a:b, 0:D], lin, SLOPE, lin, ALU.mult, ALU.max))

        y1 = {}
        hsave = [work[:, 4096 + n * 256:4096 + (n + 1) * 256].rearrange("p (w d) -> p w d", d=D) for n in range(2)]

        def ac_copy(q, dest, source):
            return ve.did(nc.vector.tensor_copy(dest, source))

        def turn_h(q):
            pe.wait(h1[q] if node_here else h_ready(q), *([c2[q - 2]] if q >= 2 else []))
            for j, w in enumerate(range(*quads[q])):
                t2[q] = pe.did(nc.tensor.transpose(bank[4 + q % 2][0:D, j * P:(j + 1) * P], hr[:, w, 0:D], ident[:, :]))

        def copy_h(q):
            n = (quads[q][1] - quads[q][0]) * P
            ac.wait(t2[q], *([ab[q - 2]] if q >= 2 else []))
            c2[q] = ac.did(nc.scalar.copy(feat[q % 2][0:D, 0:n], bank[4 + q % 2][0:D, 0:n]))

        def project(q):
            pe.wait(c2[q], ones_row, edge_here, *([cp[q - 2], r1[q - 2]] if q >= 2 else []))
            for j in range(quads[q][1] - quads[q][0]):
                ab[q] = pe.did(nc.tensor.matmul(bank[6 + q % 2][:, j * P:(j + 1) * P], feat[q % 2][:, j * P:(j + 1) * P],
                                                wedge[:, :], start=True, stop=True))

        def split(q):
            a, b = quads[q]
            both = bank[6 + q % 2][:, 0:(b - a) * P].rearrange("p (w c) -> p w c", c=P)
            part = [b_part[:, a:b, k * D:(k + 1) * D] for k in range(3)]
            r, s = rest[q % 2][:, 0:b - a, :], rest2[q % 2][:, 0:b - a, :]
            ac.wait(ab[q], *([st[q - 4]] if q >= 4 else []))
            b1[q] = ac.did(nc.scalar.copy(part[0], both[:, :, D:2 * D]))
            cp[q] = ac.did(nc.scalar.copy(a_out[q % 4][:, 0:b - a, :], both[:, :, 0:D]))
            ve.wait(cp[q])
            r1[q] = ve.did(nc.vector.tensor_tensor(r, both[:, :, D:2 * D], part[0], ALU.subtract))
            ve.wait(r1[q])
            done = ve.did(nc.vector.tensor_copy(part[1], r))
            ve.wait(done)
            b3[q] = ve.did(nc.vector.tensor_tensor(part[2], r, part[1], ALU.subtract))
            st[q] = store(table, q % 4, (a, b), a_out[q % 4][:, 0:b - a, :], cp[q])

        stages = ([turn_both, copy_both, update, activate] if node_here else []) + \
            ([turn_h, copy_h, project, split] if edge_here else [])
        staged(len(quads), stages)
        last = len(quads) - 1
        return [b3[last], cp[last], (pe.sem, pe.count)] + [(s_t[n], stores[n]) for n in range(4)] if edge_here else [h1[last]]

    s_t += [sem(f"s_table{n}") for n in (2, 3)]
    stores += [0, 0]

    xt_free = (pe.sem, pe.count)
    for lane in (ve, po, ac):
        lane.wait(xt_free)
    start_points = table_here + [pt["bank7"], (s_pw, 16), (pe.sem, pe.count), (ve.sem, ve.count)]
    edge_pass(0, tables[0], start_points, False)
    wt_zero = ve.did(nc.vector.memset(wtraj[:, :], 0.0))
    nc.sync.wait_ge(*wt_zero)
    edge_here = load_layer(0, None)
    for c in range(NW // ROWS):
        normed = attention_out(c)
    ready = dense(None, edge_here, lambda q: normed, tables[1])
    for layer in range(LAYERS):
        edge_pass(1 + layer, tables[(layer + 1) % 2], ready, True)
        node_here = load_node(layer)
        more = layer + 1 < LAYERS
        edge_here = load_layer(layer + 1, None) if more else None
        node_here = (s_lw, lw[0])
        for c in range(NW // ROWS):
            a, b = c * ROWS, (c + 1) * ROWS
            summed = ve.did(nc.vector.tensor_tensor(hr[:, a:b, D:2 * D], hr[:, a:b, D:2 * D], red1[:, a:b, :], ALU.add))
        ready = dense(node_here, edge_here, lambda q: summed, tables[layer % 2])

    s_out = sem("s_out")
    ve.wait(*ready)
    for c in range(NW // ROWS):
        a, b = c * ROWS, (c + 1) * ROWS
        tmp = work[:, 1024:1024 + ROWS * D].rearrange("p (w d) -> p w d", d=D)
        value = hr[:, a:b, 0:D]
        done = ve.did(nc.vector.tensor_tensor(value, value, x1[:, a:b, :], ALU.add))
        ve.wait(done)
        done = normalise(value, ROWS, red1[:, a:b, :], work[:, 2048:2048 + 2 * ROWS], tmp)
        nc.sync.wait_ge(*done)
        whole = min(b, NW - 1)
        nc.sync.dma_start(out[a * P:whole * P, :].rearrange("(w p) d -> p w d", p=P), red1[:, a:whole, :]).then_inc(s_out, 16)
    nc.sync.dma_start(out[full:N, :], red1[0:TAIL, NW - 1, :]).then_inc(s_out, 16)
    nc.sync.wait_ge(s_out, 16 * (NW // ROWS + 1))
    ctx.close()


def kernel(**inputs):
    import concourse.bacc as bacc
    from concourse.bass_utils import run_bass_kernel_spmd

    get = lambda n: np.asarray(inputs[n])
    arrays = {n: np.ascontiguousarray(get(n)) for n in ("x", "src", "dst", "edge_weight")}
    arrays["w_head"] = np.ascontiguousarray(get("L0_gnn_Wh").transpose(1, 0, 2).reshape(D, H * D))
    arrays["w_out"] = np.ascontiguousarray(get("L0_gnn_weight").reshape(H, D, D).transpose(1, 0, 2).reshape(D, H * D))
    edge, node = ([get(f"L1_gnn_{k}{n}") for n in range(LAYERS)] for k in ("We", "Wn"))
    be, bn = ([get(f"L1_gnn_{k}{n}") for n in range(LAYERS)] for k in ("be", "bn"))
    arrays["w_edge"] = np.stack([np.concatenate([w[:, :D].T, w[:, D:2 * D].T], axis=1) for w in edge])
    arrays["b_edge"] = np.stack([np.concatenate([np.zeros_like(b), b])[None] for b in be])
    arrays["w_traj"] = np.stack([w[:, 2 * D][None] for w in edge])
    arrays["w_node"] = np.stack([w.T for w in node])
    arrays["b_node"] = np.stack([b[None] for b in bn])
    nc = bacc.Bacc("TRN2", target_bir_lowering=False, num_devices=1)
    feed, args = {}, []
    for name, a in arrays.items():
        a = np.ascontiguousarray(a)
        feed[f"in_{name}"] = a
        args.append(nc.dram_tensor(f"in_{name}", a.shape, mybir.dt.from_np(a.dtype), kind="ExternalInput").ap())
    args.append(nc.dram_tensor("out_0", (N, D), F32, kind="ExternalOutput").ap())
    build(nc, *args)
    r = run_bass_kernel_spmd(nc, [feed], core_ids=[0])
    return r.results[0]["out_0"]
```

```python
import itertools

import numpy as np
import concourse.bass as bass
from concourse import mybir
from contextlib import ExitStack

F32, I32, I16, BF16 = mybir.dt.float32, mybir.dt.int32, mybir.dt.int16, mybir.dt.bfloat16
ALU = mybir.AluOpType
ACT = mybir.ActivationFunctionType
AX = mybir.AxisListType

P = 128
N, D, H, E = 12500, 64, 4, 400000
LAYERS = 3
EPS = 1e-5
SLOPE = 0.01
WORK = 10784
NW = -(-N // P)
TAIL = N - (NW - 1) * P
ET = E // P
G = 8
BUF = 4
GROUPS = -(-(ET + NW - 1) // G)
LAPS = GROUPS // BUF - 1
KB = -(-GROUPS * G // P)
PAIRS = KB * P
assert ET * P == E and G * D == 512


class Lane:

    def __init__(self, engine, sem):
        self.engine, self.sem, self.count = engine, sem, 0

    def did(self, instruction):
        self.count += 1
        instruction.then_inc(self.sem, 1)
        return self.sem, self.count

    def wait(self, *points):
        for sem, value in points:
            self.engine.wait_ge(sem, value)


def staged(count, stages):
    for t in range(count + len(stages) - 1):
        for s in reversed(range(len(stages))):
            if 0 <= t - s < count:
                stages[s](t - s)


def over(ap, axis, count):
    shape = list(ap.shape)
    shape.insert(axis, count)
    return ap.unsqueeze(axis).broadcast_to(shape)


def build(nc, x, src, dst, edge_weight, w_head, w_out, w_edge, b_edge, w_traj, w_node, b_node, out):
    ctx = ExitStack()

    def sb(name, shape, dt=F32):
        return ctx.enter_context(nc.sbuf_tensor(name, shape, dt))

    def sem(name):
        return ctx.enter_context(nc.semaphore(name))

    def dram(name, shape, dt):
        return nc.dram_tensor(name, shape, dt).ap()

    e_src, e_dst, e_wt = (dram(n, [ET, P], I32) for n in ("e_src", "e_dst", "e_wt"))
    tile_last = dram("tile_last", [1, ET], I32)
    pair_wt = dram("pair_wt", [PAIRS, P], I32)
    tables = [dram(f"table{n}", [NW * P, D], F32) for n in range(2)]

    hr = sb("hr", [P, NW, 2 * D])
    red1 = sb("red1", [P, NW, D])
    x1 = sb("x1", [P, NW, D])
    aux = sb("aux", [P, NW * 3 * D // 2])
    b_part = aux[:, :].bitcast(BF16).rearrange("p (w c) -> p w c", c=3 * D)
    pair_src = sb("pair_src", [P, PAIRS], I16)
    pair_dst = sb("pair_dst", [P, PAIRS], BF16)
    pair_win = sb("pair_win", [1, PAIRS], I16)
    ident = sb("ident", [P, P])
    ones = sb("ones", [P, P])
    lane_iota = sb("lane_iota", [P, P], BF16)
    whead = sb("whead", [D, H * D])
    wout = sb("wout", [D, H * D])
    wedge = sb("wedge", [D + 1, 2 * D])
    wnode = sb("wnode", [P, D])
    bnode = sb("bnode", [1, D])
    wtraj = [sb(f"wtraj{n}", [G, G * D]) for n in range(2)]
    marker = sb("marker", [1, 1])
    work = sb("work", [P, WORK])

    at = 0

    def cut(cols, dt=F32):
        nonlocal at
        ap = work[:, at:at + cols]
        at += cols
        return ap if dt is F32 else ap.bitcast(dt)

    gathered = [cut(G * D).rearrange("p (j d) -> p j d", d=D) for _ in range(BUF)]
    gather_idx = [cut(G, I32) for _ in range(BUF)]
    onehot = [cut(G * P).rearrange("p (j n) -> p j n", n=P) for _ in range(BUF)]
    b_win = [cut(G * 3 * D // 2, BF16).rearrange("p (j c) -> p j c", c=3 * D) for _ in range(2)]
    onehot_t = [cut(G * P // 2, BF16) for _ in range(2)]
    msg = [cut(G * D) for _ in range(2)]
    traj = [cut(P)[0:G, :] for _ in range(BUF)]
    assert at <= WORK, at

    bank = [ctx.enter_context(nc.psum_tensor(f"bank{n}", [P, 512], F32)) for n in range(8)]

    ve = Lane(nc.vector, sem("vector_steps"))
    ac = Lane(nc.scalar, sem("scalar_steps"))
    pe = Lane(nc.tensor, sem("tensor_steps"))
    po = Lane(nc.gpsimd, sem("pool_steps"))

    def dma(engine, dest, source, s, already=0):
        engine.dma_start(dest, source).then_inc(s, 16)
        return s, already + 16

    s_x, s_w = sem("s_x"), sem("s_w")
    tail_zero = ve.did(nc.vector.memset(hr[:, NW - 1, 0:D], 0.0))
    full = (NW - 1) * P
    nc.sync.dma_start(hr[:, 0:NW - 1, 0:D], x[0:full, :].rearrange("(w p) d -> p w d", p=P)).then_inc(s_x, 16)
    nc.sync.wait_ge(*tail_zero)
    nc.sync.dma_start(hr[0:TAIL, NW - 1, 0:D], x[full:N, :]).then_inc(s_x, 16)
    nc.scalar.dma_start(whead[:, :], w_head).then_inc(s_w, 16)
    nc.scalar.dma_start(wout[:, :], w_out).then_inc(s_w, 16)
    x_here, w_here = (s_x, 32), (s_w, 32)

    one = po.did(nc.gpsimd.memset(ones[:, :], 1.0))
    zero = po.did(nc.gpsimd.memset(ident[:, :], 0.0))
    upto = work[:, 7040:7168]
    neg_tail = work[:, 7168:7169]
    iota_i = work[:, 7170:7171].bitcast(I32)
    bound = work[:, 7172:7174]
    bound_i = work[:, 7174:7176].bitcast(I32)
    pair_of = work[:, 7176:7176 + KB]
    pair_of_i = work[:, 7204:7204 + KB].bitcast(I32)
    lane_i = work[:, 7240:7368].bitcast(I32)
    po.wait(one, zero)
    ident_ok = po.did(nc.gpsimd.affine_select(out=ident[:, :], in_=ident[:, :], compare_op=ALU.not_equal, fill=1.0,
                                              base=0, pattern=[[-1, P]], channel_multiplier=1))
    upto_ok = po.did(nc.gpsimd.affine_select(out=upto, in_=ones[:, :], compare_op=ALU.is_ge, fill=0.0,
                                             base=0, pattern=[[1, P]], channel_multiplier=-1))
    po.did(nc.gpsimd.memset(neg_tail, 0.0))
    po.wait((po.sem, po.count))
    po.did(nc.gpsimd.affine_select(out=neg_tail, in_=neg_tail, compare_op=ALU.is_ge, fill=-1e30,
                                   base=TAIL - 1, pattern=[[0, 1]], channel_multiplier=-1))
    po.did(nc.gpsimd.iota(bound_i, pattern=[[P, 2]], base=0, channel_multiplier=P))
    po.did(nc.gpsimd.iota(pair_of_i, pattern=[[P, KB]], base=0, channel_multiplier=1))
    consts = po.did(nc.gpsimd.iota(lane_i, pattern=[[1, P]], base=0, channel_multiplier=0))
    ve.wait(consts)
    ve.did(nc.vector.tensor_copy(bound, bound_i))
    ve.did(nc.vector.tensor_copy(pair_of, pair_of_i))
    vconst = ve.did(nc.vector.tensor_copy(lane_iota[:, :], lane_i))

    s_e = sem("s_edges")
    for dest, source in ((e_dst, dst), (e_src, src), (e_wt, edge_weight.bitcast(I32))):
        nc.scalar.dma_start(dest, source.rearrange("(t p) -> t p", p=P)).then_inc(s_e, 16)
    edges_here = (s_e, 48)

    ROW = 25 * P
    n_rows = E // ROW
    s_order = sem("s_order")
    order_rows = aux[0:n_rows, 0:ROW].bitcast(I32)
    falls = aux[0:n_rows, ROW:2 * ROW]
    seams = aux[0:n_rows - 1, 2 * ROW:2 * ROW + 2].bitcast(I32)
    row_falls = work[:, 0:1]
    unsorted = work[0:1, 2:3].bitcast(I32)
    nc.sync.dma_start(order_rows, dst.rearrange("(r e) -> r e", e=ROW)).then_inc(s_order, 16)
    inner = dst[ROW - 1:(n_rows - 1) * ROW + ROW - 1]
    nc.sync.dma_start(seams, inner.rearrange("(r e) -> r e", e=ROW)[0:n_rows - 1, 0:2]).then_inc(s_order, 16)
    zero_falls = ve.did(nc.vector.memset(row_falls, 0.0))
    last_zero = ve.did(nc.vector.memset(falls[:, ROW - 1:ROW], 0.0))
    ve.wait((s_order, 32), last_zero)
    ve.did(nc.vector.tensor_tensor(falls[0:n_rows - 1, ROW - 1:ROW], seams[:, 1:2], seams[:, 0:1], ALU.is_lt))
    done = ve.did(nc.vector.tensor_tensor(falls[:, 0:ROW - 1], order_rows[:, 1:ROW], order_rows[:, 0:ROW - 1], ALU.is_lt))
    ve.wait(done, zero_falls)
    done = ve.did(nc.vector.tensor_reduce(row_falls[0:n_rows, :], falls, AX.X, ALU.add))
    pe.wait(done, one)
    done = pe.did(nc.tensor.matmul(bank[0][:, 0:1], ones[:, :], row_falls, start=True, stop=True))
    ve.wait(done)
    order_known = ve.did(nc.vector.tensor_copy(unsorted, bank[0][0:1, 0:1]))

    LOT = 25
    lots = E // (P * LOT)
    lot_dst, lot_src, lot_wt = (work[:, 32 * n:32 * n + LOT] for n in range(1, 4))
    win_i, win_f = work[:, 128:128 + LOT].bitcast(I32), work[:, 160:160 + LOT]
    place, place_i = work[:, 192:192 + LOT], work[:, 224:224 + LOT].bitcast(I32)
    counts, counts_t = work[:, 256:256 + NW], work[0:NW, 360:488]
    masked = work[:, 488:488 + NW]
    before, not_before = work[:, 600:728], work[:, 728:856]
    in_win = work[:, 856:856 + LOT * NW].rearrange("p (j w) -> p j w", w=NW)
    by_lot = lambda ap: ap.rearrange("(t p j) -> t p j", p=P, j=LOT)
    spread = [(lot_dst, e_dst, by_lot(dst)), (lot_src, e_src, by_lot(src)), (lot_wt, e_wt, by_lot(edge_weight.bitcast(I32)))]
    ve.wait(upto_ok, ident_ok)
    done = ve.did(nc.vector.tensor_tensor(before, upto, ident[:, :], ALU.subtract))
    ve.wait(done)
    before_ok = ve.did(nc.vector.tensor_tensor(not_before, ones[:, :], before, ALU.subtract))
    s_cl, s_cw, s_cp, s_base, s_pl, s_pw, s_tri, s_col, s_put, s_ve, s_grouped = (
        sem("group_" + n) for n in ("count_load", "count_onehot", "counted", "base", "load", "onehot", "prefix",
                                    "column", "place", "vector", "over"))
    s_stored = [sem(f"group_stored{n}") for n in range(3)]
    block = nc.Block()
    block.__enter__()

    def if_unsorted(engine, body):
        engine.wait_ge(*order_known)
        engine.wait_ge(*edges_here)
        flag = engine.alloc_register("unsorted")
        engine.load(flag, unsorted)
        with engine.If(engine.snap(flag, min_val=0, max_val=E) > 0):
            body(engine)

    def group_load(syn):
        def count_load(t):
            syn.dma_start(lot_dst.bitcast(I32), by_lot(dst)[bass.ds(t, 1), :, :].rearrange("t p j -> (t p) j")).then_inc(s_cl, 16)

        def lot_load(t):
            for lot, _, source in spread:
                syn.dma_start(lot.bitcast(I32), source[bass.ds(t, 1), :, :].rearrange("t p j -> (t p) j")).then_inc(s_pl, 16)

        count_load(0)
        with syn.Fori(1, lots) as t:
            syn.wait_ge(s_cw, t)
            count_load(t)
        syn.wait_ge(s_cw, lots)
        lot_load(0)
        with syn.Fori(1, lots) as t:
            for s_one in s_stored:
                syn.wait_ge(s_one, t * (16 * LOT))
            lot_load(t)

    def group_vector(vec):
        def window_onehots(done, after):
            vec.tensor_scalar(win_i, lot_dst.bitcast(I32), 7, None, ALU.arith_shift_right).then_inc(s_ve, 1)
            vec.wait_ge(s_ve, done + 1)
            vec.tensor_copy(win_f, win_i).then_inc(s_ve, 1)
            vec.wait_ge(s_ve, done + 2)
            vec.tensor_tensor(in_win, over(lane_iota[:, 0:NW], 1, LOT), over(win_f, 2, NW), ALU.is_equal).then_inc(after, 1)

        with vec.Fori(0, lots) as t:
            vec.wait_ge(s_cl, (t + 1) * 16)
            vec.wait_ge(s_cp, t + 1)
            window_onehots(t * 2, s_cw)
        vec.wait_ge(s_cp, lots + 1)
        vec.tensor_copy(counts, bank[0][:, 0:NW]).then_inc(s_base, 1)
        vec.wait_ge(s_base, 2)
        vec.tensor_copy(counts_t, bank[1][0:NW, 0:P]).then_inc(s_base, 1)
        per_lot = 2 + LOT + 1
        with vec.Fori(0, lots) as t:
            vec.wait_ge(s_cp, t + (lots + 1))
            vec.wait_ge(s_pl, (t + 1) * 48)
            window_onehots(t * per_lot + 2 * lots, s_pw)
            for j in range(LOT):
                vec.wait_ge(s_tri, t * LOT + (j + 1))
                vec.wait_ge(s_pw, t + 1)
                vec.wait_ge(s_ve, t * per_lot + (2 * lots + 2 + j))
                vec.tensor_tensor(masked, in_win[:, j, :], bank[2][:, 0:NW], ALU.mult).then_inc(s_col, 1)
                vec.wait_ge(s_col, t * LOT + (j + 1))
                vec.tensor_reduce(place[:, j:j + 1], masked, AX.X, ALU.add).then_inc(s_ve, 1)
            vec.wait_ge(s_ve, t * per_lot + (2 * lots + 2 + LOT))
            vec.tensor_copy(place_i, place).then_inc(s_ve, 1)
            vec.wait_ge(s_ve, t * per_lot + (2 * lots + per_lot))
            vec.sem_inc(s_put, 1)

    def group_tensor(ten):
        ten.matmul(bank[0][:, 0:NW], ident[:, :], in_win_zero, start=True, stop=False, skip_group_check=True).then_inc(s_cp, 1)
        with ten.Fori(0, lots) as t:
            ten.wait_ge(s_cw, t + 1)
            for j in range(LOT):
                last = ten.matmul(bank[0][:, 0:NW], ones[:, :], in_win[:, j, :], start=False, stop=False, skip_group_check=True)
            last.then_inc(s_cp, 1)
        ten.wait_ge(s_base, 1)
        ten.transpose(bank[1][0:NW, 0:P], counts, ident[:, :]).then_inc(s_base, 1)
        ten.wait_ge(s_base, 3)
        ten.matmul(bank[2][:, 0:NW], counts_t, before[0:NW, 0:NW], start=True, stop=False, skip_group_check=True)
        with ten.Fori(0, lots) as t:
            ten.wait_ge(s_pw, t + 1)
            for j in range(LOT):
                ten.matmul(bank[2][:, 0:NW], before, in_win[:, j, :], start=False, stop=False,
                           skip_group_check=True).then_inc(s_tri, 1)
                ten.wait_ge(s_col, t * LOT + (j + 1))
                last = ten.matmul(bank[2][:, 0:NW], not_before, in_win[:, j, :], start=False, stop=False,
                                  skip_group_check=True)
            last.then_inc(s_cp, 1)

    def group_pool(pool):
        with pool.Fori(0, lots) as t:
            pool.wait_ge(s_put, t + 1)
            pool.sem_inc(s_grouped, 1)
            for j in range(LOT):
                for s_one, (lot, dest, _) in zip(s_stored, spread):
                    pool.indirect_dma_start(dest.rearrange("t (p o) -> (t p) o", o=1),
                                            bass.IndirectOffsetOnAxis(ap=place_i[:, j:j + 1], axis=0),
                                            lot[:, j:j + 1].bitcast(I32), None).then_inc(s_one, 16)
        for s_one in s_stored:
            pool.wait_ge(s_one, lots * 16 * LOT)
        pool.sem_inc(s_grouped, 1)

    zero_in = ve.did(nc.vector.memset(masked, 0.0))
    in_win_zero = masked

    block.sync(lambda e: if_unsorted(e, group_load))
    block.vector(lambda e: if_unsorted(e, group_vector))
    block.tensor(lambda e: (e.wait_ge(*zero_in), e.wait_ge(*before_ok), if_unsorted(e, group_tensor)))
    block.gpsimd(lambda e: if_unsorted(e, group_pool))
    block.__exit__(None, None, None)
    edges_here = po.did(nc.gpsimd.memset(marker[:, :], 0.0))

    last_i = aux[0:NW, 0:ET].bitcast(I32)
    below = aux[0:NW, ET:2 * ET]
    past = aux[0:NW, 0:PAIRS]
    win_base = aux[:, PAIRS:2 * PAIRS]
    edge_rows = [aux[:, 2 * PAIRS + n * 512:2 * PAIRS + (n + 1) * 512] for n in range(4)]
    small = work[:, 7370:7430]
    tile_of = work[:, 7440:7440 + KB].bitcast(I32)
    lo_hi_rows = work[0:NW, 6528:6784].bitcast(I32)
    lo_hi_below = work[0:NW, 6784:7040]
    pair_iota_i = x1[0:NW, 0:52, :].rearrange("p w d -> p (w d)")
    col = lambda n: small[0:NW, n:n + 1]
    full_tiles, first_idx = small[0:NW, 0:2], small[0:NW, 2:4]
    first_idx_i = small[0:NW, 4:6].bitcast(I32)
    inside = small[0:NW, 6:8]
    start = small[0:NW, 8:10]
    is_full, is_none = small[0:NW, 10:12], small[0:NW, 12:14]
    first_tile = small[0:NW, 14:16]
    last_tile, nonempty, pairs = col(16), col(17), col(18)
    one_delta = small[0:NW, 20:22]
    pairs_upto = col(22)
    pt = {}
    s_last, s_rows = sem("s_last"), sem("s_rows")

    def find_lasts():
        nc.sync.wait_ge(*edges_here)
        nc.sync.dma_start(aux[0:125, 0:25].bitcast(I32),
                          e_dst[:, P - 1:P].rearrange("(a b) o -> a (b o)", b=25),
                          allow_slow_non_contiguous=True).then_inc(s_last, 16)
        nc.sync.wait_ge(s_last, 16)
        nc.sync.dma_start(tile_last[0, :].rearrange("(a b) -> a b", b=25), aux[0:125, 0:25].bitcast(I32)).then_inc(s_last, 16)
        nc.sync.wait_ge(s_last, 32)
        nc.sync.dma_start(last_i, tile_last[0:1, :].broadcast_to([NW, ET])).then_inc(s_last, 16)

    def count_full():
        ve.wait((s_last, 48), vconst)
        for b in range(2):
            done = ve.did(nc.vector.tensor_scalar(below, last_i, bound[0:NW, b:b + 1], None, ALU.is_lt))
            ve.wait(done)
            done = ve.did(nc.vector.tensor_reduce(full_tiles[:, b:b + 1], below, AX.X, ALU.add))
            ve.wait(done)
        done = ve.did(nc.vector.tensor_scalar(first_idx, full_tiles, float(ET - 1), None, ALU.min))
        ve.wait(done)
        pt["idx"] = ve.did(nc.vector.tensor_copy(first_idx_i, first_idx))
        po.wait(pt["idx"])
        for b in range(2):
            nc.gpsimd.indirect_dma_start(lo_hi_rows[:, b * P:(b + 1) * P], None, e_dst,
                                         bass.IndirectOffsetOnAxis(ap=first_idx_i[:, b:b + 1], axis=0)).then_inc(s_rows, 16)

    def count_pairs():
        ve.wait((s_rows, 32))
        for b in range(2):
            done = ve.did(nc.vector.tensor_scalar(lo_hi_below[:, b * P:(b + 1) * P], lo_hi_rows[:, b * P:(b + 1) * P],
                                                  bound[0:NW, b:b + 1], None, ALU.is_lt))
        ve.wait(done)
        done = ve.did(nc.vector.tensor_reduce(inside, lo_hi_below.rearrange("p (b e) -> p b e", b=2), AX.X, ALU.add))
        ve.wait(done)
        ve.did(nc.vector.scalar_tensor_tensor(start, first_idx, float(P), inside, ALU.mult, ALU.add))
        ve.did(nc.vector.tensor_scalar(is_full, inside, float(P), None, ALU.is_equal))
        done = ve.did(nc.vector.tensor_scalar(is_none, inside, 0.0, None, ALU.is_equal))
        ve.wait(done)
        ve.did(nc.vector.tensor_tensor(first_tile, first_idx, is_full, ALU.add))
        ve.did(nc.vector.tensor_tensor(last_tile, first_idx[:, 1:2], is_none[:, 1:2], ALU.subtract))
        done = ve.did(nc.vector.tensor_tensor(nonempty, start[:, 1:2], start[:, 0:1], ALU.is_gt))
        ve.wait(done)
        done = ve.did(nc.vector.tensor_tensor(pairs, last_tile, first_tile[:, 0:1], ALU.subtract))
        ve.wait(done)
        done = ve.did(nc.vector.scalar_tensor_tensor(pairs, pairs, 1.0, nonempty, ALU.add, ALU.mult))
        ve.wait(done)
        done = ve.did(nc.vector.tensor_tensor(one_delta[:, 1:2], first_tile[:, 1:2], first_tile[:, 0:1], ALU.subtract))
        ve.wait(done)
        ve.did(nc.vector.memset(one_delta[:, 0:1], 1.0))
        pt["pairs"] = ve.did(nc.vector.tensor_tensor(one_delta[:, 1:2], one_delta[:, 1:2], pairs, ALU.subtract))

    def sum_pairs():
        pe.wait(pt["pairs"], upto_ok, pt["bank7"])
        done = pe.did(nc.tensor.matmul(bank[7][0:NW, 0:1], upto[0:NW, 0:NW], pairs, start=True, stop=True))
        ve.wait(done)
        done = ve.did(nc.vector.tensor_copy(pairs_upto, bank[7][0:NW, 0:1]))
        po.wait(pt["idx"])
        done_i = po.did(nc.gpsimd.iota(win_base[0:NW, :].bitcast(I32), pattern=[[1, PAIRS]], base=0, channel_multiplier=0))
        ve.wait(done, done_i)
        pt["past"] = ve.did(nc.vector.tensor_scalar(past, win_base[0:NW, :].bitcast(I32), pairs_upto, None, ALU.is_ge))

    def place_pairs():
        pe.wait(pt["past"], pt["bank7"])
        for b in range(KB):
            done = pe.did(nc.tensor.matmul(bank[7][:, 2 * b:2 * b + 2], past[:, b * P:(b + 1) * P], one_delta,
                                           start=True, stop=True))
        tiles = small[:, 30:30 + KB]
        ve.wait(done)
        done = ve.did(nc.vector.tensor_tensor(tiles, bank[7][:, 0:2 * KB].rearrange("p (b c) -> p b c", c=2)[:, :, 1],
                                              pair_of, ALU.add))
        ve.wait(done)
        pt["tiles"] = ve.did(nc.vector.tensor_scalar(tile_of, tiles, float(ET - 1), None, ALU.min))
        for c in range(-(-PAIRS // 512)):
            a, b = c * 512, min((c + 1) * 512, PAIRS)
            pe.wait(pt["tiles"] if c == 0 else done)
            summed = pe.did(nc.tensor.matmul(bank[7][:, 0:b - a], ones[0:NW, :], past[:, a:b], start=True, stop=True))
            ve.wait(summed)
            ve.did(nc.vector.tensor_scalar(win_base[:, a:b], bank[7][:, 0:b - a], float(P), None, ALU.mult))
            done = ve.did(nc.vector.tensor_scalar(pair_win[:, a:b], bank[7][0:1, 0:b - a], float(NW - 1), None, ALU.min))
        pt["win"] = pt["bank7"] = done

    s_er = [sem(f"s_edge_rows{n}") for n in range(4)]
    rows_read = [None] * 4
    uses = [0] * 4

    def edge_columns(c):
        batches = list(range(4 * c, min(4 * c + 4, KB)))
        width = P * len(batches)
        for which, table in ((0, e_dst), (1, e_src)):
            n = 2 * (c % 2) + which
            rows = edge_rows[n]
            po.wait(pt["tiles"])
            if rows_read[n]:
                po.wait(*rows_read[n])
            for j, b in enumerate(batches):
                nc.gpsimd.indirect_dma_start(rows[:, j * P:(j + 1) * P].bitcast(I32), None, table,
                                             bass.IndirectOffsetOnAxis(ap=tile_of[:, b:b + 1], axis=0)).then_inc(s_er[n], 16)
            uses[n] += 16 * len(batches)

    def turn_columns(c):
        batches = list(range(4 * c, min(4 * c + 4, KB)))
        width = P * len(batches)
        for which in (0, 1):
            n = 2 * (c % 2) + which
            rows = edge_rows[n][:, 0:width]
            ve.wait((s_er[n], turned[c][which]))
            as_float = ve.did(nc.vector.tensor_copy(rows, rows.bitcast(I32)))
            pe.wait(as_float, pt["bank7"])
            for j in range(len(batches)):
                done = pe.did(nc.tensor.transpose(bank[7][:, j * P:(j + 1) * P], rows[:, j * P:(j + 1) * P], ident[:, :]))
            rows_read[n] = [done]
            ve.wait(done, pt["win"])
            a = 4 * c * P
            if which == 0:
                pt["bank7"] = ve.did(nc.vector.tensor_tensor(pair_dst[:, a:a + width], bank[7][:, 0:width],
                                                             win_base[:, a:a + width], ALU.subtract))
            else:
                pt["bank7"] = ve.did(nc.vector.tensor_copy(pair_src[:, a:a + width], bank[7][:, 0:width]))

    turned = {}

    def columns_step(c):
        if c < -(-KB // 4):
            edge_columns(c)
            turned[c] = (uses[2 * (c % 2)], uses[2 * (c % 2) + 1])
        if c > 0:
            turn_columns(c - 1)

    scores = work[:, 0:NW * H].rearrange("p (w h) -> p w h", h=H)
    attn = work[:, 400:400 + NW * H].rearrange("p (w h) -> p w h", h=H)
    prod = [work[:, 800 + n * 512:1312 + n * 512] for n in range(2)]
    half = NW // 2

    def xt(w):
        home = x1 if w < half else red1
        return home[0:D, :, :].rearrange("p w d -> p (w d)")[:, (w % half) * P:(w % half + 1) * P]

    assert 2 * half == NW and half * P == NW * D
    chunk = [(w, w + 2) for w in range(0, NW, 2)]
    turned_x, copied_x, headed, mixed = {}, {}, {}, {}
    pt["bank7"] = ident_ok

    def turn_x(c):
        pe.wait(x_here, ident_ok, *([copied_x[c - 2]] if c >= 2 else []))
        for j, w in enumerate(range(*chunk[c])):
            turned_x[c] = pe.did(nc.tensor.transpose(bank[c % 2][0:D, j * P:(j + 1) * P], hr[:, w, 0:D], ident[:, :]))

    def copy_x(c):
        ac.wait(turned_x[c])
        for j, w in enumerate(range(*chunk[c])):
            copied_x[c] = ac.did(nc.scalar.copy(xt(w), bank[c % 2][0:D, j * P:(j + 1) * P]))

    def head_x(c):
        pe.wait(w_here, copied_x[c], *([mixed[c - 2]] if c >= 2 else []))
        for j, w in enumerate(range(*chunk[c])):
            headed[c] = pe.did(nc.tensor.matmul(bank[2 + c % 2][:, j * H * D:(j + 1) * H * D], xt(w), whead[:, :],
                                                start=True, stop=True))

    def score_x(c):
        a, b = chunk[c]
        ve.wait(headed[c])
        mixed[c] = ve.did(nc.vector.tensor_tensor(
            prod[c % 2].rearrange("p (w h d) -> p w h d", h=H, d=D),
            bank[2 + c % 2][:, :].rearrange("p (w h d) -> p w h d", h=H, d=D), over(hr[:, a:b, 0:D], 2, H), ALU.mult))
        ve.wait(mixed[c])
        return ve.did(nc.vector.tensor_reduce(scores[:, a:b, :], prod[c % 2].rearrange("p (w h d) -> p w h d", h=H, d=D),
                                              AX.X, ALU.add))

    steps = {2: find_lasts, 14: count_full, 19: count_pairs, 23: sum_pairs, 27: place_pairs}
    for n in range(-(-KB // 4) + 1):
        steps[33 + 2 * n] = lambda n=n: columns_step(n)
    last_score = {}

    def score_step(c):
        last_score[0] = score_x(c)
        if c in steps:
            steps[c]()

    staged(len(chunk), [turn_x, copy_x, head_x, score_step])

    ve.wait(last_score[0], consts)
    done = ve.did(nc.vector.tensor_scalar(scores[:, NW - 1, :], scores[:, NW - 1, :], neg_tail, None, ALU.add))
    ve.wait(done)
    top = work[:, 1824:1828]
    top_t, diag, neg_top = work[0:H, 1830:1831], work[0:H, 1832:1836], work[:, 1836:1840]
    total, inverse = work[:, 1840:1844], work[:, 1844:1848]
    done = ve.did(nc.vector.tensor_reduce(top, scores.rearrange("p w h -> p h w"), AX.X, ALU.max))
    pe.wait(done)
    done = pe.did(nc.tensor.transpose(bank[0][0:H, 0:P], top, ident[:, :]))
    ve.wait(done)
    done = ve.did(nc.vector.tensor_reduce(top_t, bank[0][0:H, 0:P], AX.X, ALU.max))
    ve.wait(done)
    done = ve.did(nc.vector.tensor_scalar(diag, ident[0:H, 0:H], top_t, None, ALU.mult))
    pe.wait(done)
    done = pe.did(nc.tensor.matmul(bank[1][:, 0:H], ones[0:H, :], diag, start=True, stop=True))
    ve.wait(done)
    scale = float(D) ** -0.5
    done = ve.did(nc.vector.tensor_scalar(neg_top, bank[1][:, 0:H], -scale, None, ALU.mult))
    ac.wait(done)
    for h in range(H):
        done = ac.did(nc.scalar.activation(attn[:, :, h], scores[:, :, h], ACT.Exp, bias=neg_top[:, h:h + 1], scale=scale))
    ve.wait(done)
    done = ve.did(nc.vector.tensor_reduce(total, attn.rearrange("p w h -> p h w"), AX.X, ALU.add))
    pe.wait(done)
    done = pe.did(nc.tensor.matmul(bank[0][:, 0:H], ones[:, :], total, start=True, stop=True))
    ve.wait(done)
    done = ve.did(nc.vector.reciprocal(inverse, bank[0][:, 0:H]))
    ve.wait(done)
    attn_ok = ve.did(nc.vector.tensor_tensor(attn, attn, over(inverse, 1, NW), ALU.mult))

    ROWS = 14
    y_out = [work[:, 1856 + n * ROWS * D:1856 + (n + 1) * ROWS * D].rearrange("p (w d) -> p w d", d=D) for n in range(2)]
    s_t = [sem(f"s_table{n}") for n in range(2)]
    stores = [0, 0]
    weighted, summed_y = {}, {}

    def store(table, n, rows, source, point):
        nc.sync.wait_ge(*point)
        nc.sync.dma_start(table[rows[0] * P:rows[1] * P, :].rearrange("(w p) d -> p w d", p=P), source).then_inc(s_t[n], 16)
        stores[n] += 16
        return s_t[n], stores[n]

    y_stored = {}

    def out_x(c):
        pe.wait(attn_ok, *([weighted[c - 2]] if c >= 2 else []))
        for j, w in enumerate(range(*chunk[c])):
            headed[c] = pe.did(nc.tensor.matmul(bank[2 + c % 2][:, j * H * D:(j + 1) * H * D], xt(w), wout[:, :],
                                                start=True, stop=True))

    def sum_y(c):
        a, b = chunk[c]
        n, part = (a // ROWS) % 2, a // ROWS
        ve.wait(headed[c], attn_ok)
        weighted[c] = ve.did(nc.vector.tensor_tensor(
            prod[c % 2].rearrange("p (w h d) -> p w h d", h=H, d=D),
            bank[2 + c % 2][:, :].rearrange("p (w h d) -> p w h d", h=H, d=D), over(attn[:, a:b, :], 3, D), ALU.mult))
        ve.wait(weighted[c])
        if part >= 2 and a % ROWS == 0:
            ve.wait(y_stored[part - 2])
        done = ve.did(nc.vector.tensor_reduce(y_out[n][:, a % ROWS:a % ROWS + b - a, :],
                                              prod[c % 2].rearrange("p (w h d) -> p w d h", h=H, d=D), AX.X, ALU.add))
        if b % ROWS == 0:
            y_stored[part] = store(tables[0], n, (part * ROWS, (part + 1) * ROWS), y_out[n], done)

    staged(len(chunk), [out_x, sum_y])
    table_here = [(s_t[0], stores[0]), (s_t[1], stores[1])]

    s_pw, s_pr = sem("s_pair_weight"), sem("s_pair_rows")
    wt_rows = aux[:, 0:PAIRS]
    po.wait(pt["win"], pt["bank7"])
    for b in range(KB):
        nc.gpsimd.indirect_dma_start(wt_rows[:, b * P:(b + 1) * P].bitcast(I32), None, e_wt,
                                     bass.IndirectOffsetOnAxis(ap=tile_of[:, b:b + 1], axis=0)).then_inc(s_pr, 16)
    nc.sync.wait_ge(s_pr, 16 * KB)
    nc.sync.dma_start(pair_wt.rearrange("(b p) e -> p b e", p=P),
                      wt_rows.bitcast(I32).rearrange("p (b e) -> p b e", e=P)).then_inc(s_pw, 16)
    pair_wt_f = pair_wt.bitcast(F32)

    def edge_pass(number, table, table_points, layered):
        name = f"pass{number}_"
        s_idx, s_oh, s_msg, s_acc, s_sc, s_tr, s_ot, s_pre, s_z, s_zc, s_go = (
            sem(name + n) for n in ("idx", "onehot", "msg", "add", "scatter", "turn", "onehot_t", "pre", "z", "z_copy", "go"))
        s_g = [sem(f"{name}gather{n}") for n in range(BUF)]
        s_tj = [sem(f"{name}traj{n}") for n in range(BUF)]
        turned = [[bank[n], bank[2 + n]] for n in range(2)]
        z_ps = [bank[4], bank[5]]
        sum_ps = [bank[6], bank[7]]
        for e in (nc.vector, nc.gpsimd, nc.tensor, nc.scalar, nc.sync):
            for point in table_points:
                e.wait_ge(*point)
        block = nc.Block()
        block.__enter__()

        def run(engine, step):
            for q in range(BUF):
                step(q, q, 0)
            with engine.Fori(1, LAPS) as i:
                for q in range(BUF):
                    step(i * BUF + q, q, i)
            for g in range(LAPS * BUF, GROUPS):
                step(g, g % BUF, g // BUF)

        def is_group(g):
            return not isinstance(g, int) or 0 <= g < GROUPS

        serial = itertools.count()

        def windows(engine, g):
            regs = [engine.alloc_register(f"{name}win{next(serial)}") for _ in range(G)]
            engine.load(regs, pair_win[0:1, bass.ds(g * G, G)])
            return [engine.snap(r, donate=True, min_val=0, max_val=NW - 1) for r in regs]

        @block.gpsimd
        def _(pool):
            def step(g, q, lap):
                pool.wait_ge(s_idx, g + 1)
                pool.sem_inc(s_go)
                for j in range(G):
                    pool.indirect_dma_start(gathered[q][:, j, :], None, table,
                                            bass.IndirectOffsetOnAxis(ap=gather_idx[q][:, j:j + 1], axis=0)
                                            ).then_inc(s_g[q], 16)
            run(pool, step)

        @block.vector
        def _(vec):
            def copy_idx(g, q):
                if is_group(g):
                    vec.tensor_copy(gather_idx[q % BUF], pair_src[:, bass.ds(g * G, G)]).then_inc(s_idx, 1)

            def make_onehot(g, q):
                if is_group(g):
                    rel = pair_dst[:, bass.ds(g * G, G)]
                    vec.tensor_tensor(onehot[q % BUF], over(lane_iota[:, :], 1, G), over(rel, 2, P),
                                      ALU.is_equal).then_inc(s_oh, 1)

            def add(g, q):
                if not is_group(g):
                    return
                win = windows(vec, g)
                vec.wait_ge(s_sc, g + 1)
                for j in range(G):
                    vec.wait_ge(s_acc, g * G + (j + 1))
                    w = bass.ds(win[j], 1)
                    home = hr[:, w, D:2 * D] if j % 2 == 0 else red1[:, w, :]
                    vec.tensor_tensor(home, home, sum_ps[q % 2][:, j * D:(j + 1) * D].unsqueeze(1),
                                      ALU.add).then_inc(s_acc, 1)

            def step(g, q, lap):
                if layered:
                    add(g - 2, q - 2)
                    make_onehot(g + 1, q + 1)
                    if is_group(g):
                        vec.wait_ge(s_zc, g + 1)
                        copy_idx(g + BUF, q)
                        vec.scalar_tensor_tensor(msg[q % 2], msg[q % 2], SLOPE, msg[q % 2],
                                                 ALU.mult, ALU.max).then_inc(s_msg, 1)
                else:
                    make_onehot(g + 1, q + 1)
                    add(g - 1, q - 1)
                    copy_idx(g + (BUF - 1), q + BUF - 1)

            vec.memset(hr[:, :, D:2 * D], 0.0).then_inc(s_acc, 1)
            vec.memset(red1[:, :, :], 0.0).then_inc(s_acc, 1)
            for g in range(BUF if layered else BUF - 1):
                copy_idx(g, g)
            make_onehot(0, 0)
            run(vec, step)
            for g in range(GROUPS, GROUPS + (2 if layered else 1)):
                add(g - (2 if layered else 1), g - (2 if layered else 1))

        @block.tensor
        def _(ten):
            def turn_onehot(g, q):
                ten.wait_ge(s_oh, g + 1)
                for j in range(G):
                    last = ten.transpose(turned[q % 2][j // 4][:, (j % 4) * P:(j % 4 + 1) * P], onehot[q % BUF][:, j, :],
                                         ident[:, :])
                last.then_inc(s_tr, 1)

            def pre_message(g, q, lap):
                ten.wait_ge(s_ot, g + 1)
                ten.wait_ge(s_tj[q % BUF], (lap + 1) * 16)
                z = z_ps[q % 2]
                ten.matmul(z[:, :], traj[q % BUF], wtraj[number % 2][:, :], start=True, stop=False, skip_group_check=True)
                for j in range(G):
                    for part in range(3):
                        last = ten.matmul(z[:, j * D:(j + 1) * D], onehot_t[q % 2][:, j * P:(j + 1) * P],
                                          b_win[q % 2][:, j, part * D:(part + 1) * D], start=False, stop=False,
                                          skip_group_check=True)
                last.then_inc(s_pre, 1)

            def scatter(g, q):
                if not is_group(g):
                    return
                for j in range(G):
                    rows = msg[q % 2][:, j * D:(j + 1) * D] if layered else gathered[q % BUF][:, j, :]
                    last = ten.matmul(sum_ps[q % 2][:, j * D:(j + 1) * D], onehot[q % BUF][:, j, :], rows,
                                      start=True, stop=True)
                last.then_inc(s_sc, 1)

            def step(g, q, lap):
                if layered:
                    if is_group(g):
                        ten.wait_ge(s_g[q], (lap + 1) * (16 * G))
                        ten.matmul(z_ps[q % 2][:, :], ident[:, :], gathered[q].rearrange("p j d -> p (j d)"),
                                   start=False, stop=True, skip_group_check=True).then_inc(s_z, 1)
                    if is_group(g - 1):
                        ten.wait_ge(s_msg, g)
                        ten.wait_ge(s_acc, (g - 2) * G + 2 if not isinstance(g, int) or g >= 2 else 2)
                        scatter(g - 1, q - 1)
                    if is_group(g + 1):
                        turn_onehot(g + 1, q + 1)
                        pre_message(g + 1, q + 1, lap + (q + 1) // BUF)
                else:
                    ten.wait_ge(s_oh, g + 1)
                    ten.wait_ge(s_g[q], (lap + 1) * (16 * G))
                    ten.wait_ge(s_acc, (g - 1) * G + 2 if not isinstance(g, int) or g >= 1 else 2)
                    scatter(g, q)

            if layered:
                turn_onehot(0, 0)
                pre_message(0, 0, 0)
            run(ten, step)
            if layered:
                ten.wait_ge(s_msg, GROUPS)
                ten.wait_ge(s_acc, (GROUPS - 2) * G + 2)
                scatter(GROUPS - 1, GROUPS - 1)

        if layered:
            @block.scalar
            def _(sca):
                def turned_and_windows(g, q):
                    if not is_group(g):
                        return
                    win = windows(sca, g)
                    if not isinstance(g, int) or g >= 2:
                        sca.wait_ge(s_pre, g - 1)
                    for j in range(G):
                        sca.copy(b_win[q % 2][:, j:j + 1, :], b_part[:, bass.ds(win[j], 1), :])
                    sca.wait_ge(s_tr, g + 1)
                    for k in range(2):
                        last = sca.copy(onehot_t[q % 2][:, k * 512:(k + 1) * 512], turned[q % 2][k][:, :])
                    last.then_inc(s_ot, 1)

                def step(g, q, lap):
                    sca.wait_ge(s_z, g + 1)
                    if not isinstance(g, int) or g >= 2:
                        sca.wait_ge(s_sc, g - 1)
                    sca.copy(msg[q % 2], z_ps[q % 2][:, :]).then_inc(s_zc, 1)
                    turned_and_windows(g + 1, q + 1)

                turned_and_windows(0, 0)
                run(sca, step)

            @block.sync
            def _(syn):
                def load_traj(g, q):
                    if is_group(g):
                        syn.dma_start(traj[q], pair_wt_f[bass.ds(g * G, G), :]).then_inc(s_tj[q], 16)

                def step(g, q, lap):
                    syn.wait_ge(s_pre, g + 1)
                    load_traj(g + BUF, q)

                for q in range(BUF):
                    load_traj(q, q)
                run(syn, step)

        block.__exit__(None, None, None)
        for e in (nc.vector, nc.scalar, nc.tensor, nc.sync, nc.gpsimd):
            e.wait_ge(s_acc, GROUPS * G + 2)

    def normalise(value, count, dest, scratch, tmp):
        mean, var = scratch[:, 0:count], scratch[:, count:2 * count]
        ve.did(nc.vector.tensor_reduce(mean, value, AX.X, ALU.add))
        ve.wait((ve.sem, ve.count))
        ve.did(nc.vector.tensor_scalar(mean, mean, 1.0 / D, None, ALU.mult))
        ve.wait((ve.sem, ve.count))
        done = ve.did(nc.vector.tensor_tensor(value, value, over(mean, 2, D), ALU.subtract))
        ac.wait(done)
        done = ac.did(nc.scalar.activation(tmp, value, ACT.Square))
        ve.wait(done)
        done = ve.did(nc.vector.tensor_reduce(var, tmp, AX.X, ALU.add))
        ve.wait(done)
        done = ve.did(nc.vector.tensor_scalar(var, var, 1.0 / D, EPS, ALU.mult, ALU.add))
        ac.wait(done)
        done = ac.did(nc.scalar.activation(var, var, ACT.Sqrt))
        ve.wait(done)
        done = ve.did(nc.vector.reciprocal(var, var))
        ve.wait(done)
        return ve.did(nc.vector.tensor_tensor(dest, value, over(var, 2, D), ALU.mult))

    def attention_out(c):
        a, b = c * ROWS, (c + 1) * ROWS
        value = work[:, 0:ROWS * D].rearrange("p (w d) -> p w d", d=D)
        tmp = work[:, 1024:1024 + ROWS * D].rearrange("p (w d) -> p w d", d=D)
        scratch = work[:, 2048:2048 + 2 * ROWS]
        sums = hr[:, a:b, D:2 * D]
        done = ve.did(nc.vector.tensor_tensor(sums, sums, red1[:, a:b, :], ALU.add))
        ve.wait(done)
        done = ve.did(nc.vector.tensor_scalar(tmp, sums, 0.0, None, ALU.min))
        ac.wait(done)
        done = ac.did(nc.scalar.activation(tmp, tmp, ACT.Exp))
        done_v = ve.did(nc.vector.scalar_tensor_tensor(value, sums, 0.0, hr[:, a:b, 0:D], ALU.max, ALU.add))
        ve.wait(done, done_v)
        done = ve.did(nc.vector.scalar_tensor_tensor(value, tmp, -1.0, value, ALU.add, ALU.add))
        ve.wait(done)
        done = normalise(value, ROWS, x1[:, a:b, :], scratch, tmp)
        ve.wait(done)
        return ve.did(nc.vector.tensor_copy(hr[:, a:b, 0:D], x1[:, a:b, :]))

    QUAD = 4
    quads = [(w, min(w + QUAD, NW)) for w in range(0, NW, QUAD)]
    s_lw = sem("s_layer_weights")
    lw = [0]

    def load_layer(layer, engine_points):
        nc.sync.dma_start(wedge[0:D, :], w_edge[layer]).then_inc(s_lw, 16)
        nc.sync.dma_start(wedge[D:D + 1, :], b_edge[layer]).then_inc(s_lw, 16)
        for j in range(G):
            nc.sync.dma_start(wtraj[(layer + 1) % 2][j:j + 1, j * D:(j + 1) * D], w_traj[layer]).then_inc(s_lw, 16)
        lw[0] += 16 * (2 + G)
        return s_lw, lw[0]

    def load_node(layer):
        nc.sync.dma_start(wnode[:, :], w_node[layer]).then_inc(s_lw, 16)
        nc.sync.dma_start(bnode[:, :], b_node[layer]).then_inc(s_lw, 16)
        lw[0] += 32
        return s_lw, lw[0]

    cat = [work[:, n * 512:(n + 1) * 512] for n in range(2)]
    feat = [work[0:D + 1, 1024 + n * 512:1024 + (n + 1) * 512] for n in range(2)]
    rest = [work[:, 2048 + n * 256:2048 + (n + 1) * 256].rearrange("p (w d) -> p w d", d=D) for n in range(2)]
    rest2 = [work[:, 2560 + n * 256:2560 + (n + 1) * 256].rearrange("p (w d) -> p w d", d=D) for n in range(2)]
    a_out = [work[:, 3072 + n * 256:3072 + (n + 1) * 256].rearrange("p (w d) -> p w d", d=D) for n in range(4)]

    def dense(node_here, edge_here, h_ready, table):
        t1, c1, u1, h1, t2, c2, ab, cp, b1, r1, b2, b3, st = ({} for _ in range(13))
        if edge_here:
            for f in feat:
                ones_row = ve.did(nc.vector.memset(f[D:D + 1, :], 1.0))

        def turn_both(q):
            pe.wait(h_ready(q), *([c1[q - 2]] if q >= 2 else []))
            for j, w in enumerate(range(*quads[q])):
                t1[q] = pe.did(nc.tensor.transpose(bank[q % 2][:, j * P:(j + 1) * P], hr[:, w, :], ident[:, :]))

        def copy_both(q):
            n = (quads[q][1] - quads[q][0]) * P
            ac.wait(t1[q], *([u1[q - 2]] if q >= 2 else []))
            c1[q] = ac.did(nc.scalar.copy(cat[q % 2][:, 0:n], bank[q % 2][:, 0:n]))

        def update(q):
            pe.wait(c1[q], node_here, *([h1[q - 2]] if q >= 2 else []))
            for j in range(quads[q][1] - quads[q][0]):
                o = bank[2 + q % 2][:, j * D:(j + 1) * D]
                pe.did(nc.tensor.matmul(o, ones[0:1, :], bnode[:, :], start=True, stop=False))
                u1[q] = pe.did(nc.tensor.matmul(o, cat[q % 2][:, j * P:(j + 1) * P], wnode[:, :], start=False, stop=True))

        def activate(q):
            a, b = quads[q]
            ve.wait(u1[q], *([y1[q - 2]] if q >= 2 else []))
            o = bank[2 + q % 2][:, 0:(b - a) * D].rearrange("p (w d) -> p w d", d=D)
            lin = rest[q % 2][:, 0:b - a, :] if not edge_here else hsave[q % 2][:, 0:b - a, :]
            y1[q] = ac_copy(q, lin, o)
            ve.wait(y1[q])
            h1[q] = ve.did(nc.vector.scalar_tensor_tensor(hr[:, a:b, 0:D], lin, SLOPE, lin, ALU.mult, ALU.max))

        y1 = {}
        hsave = [work[:, 4096 + n * 256:4096 + (n + 1) * 256].rearrange("p (w d) -> p w d", d=D) for n in range(2)]

        def ac_copy(q, dest, source):
            return ve.did(nc.vector.tensor_copy(dest, source))

        def turn_h(q):
            pe.wait(h1[q] if node_here else h_ready(q), *([c2[q - 2]] if q >= 2 else []))
            for j, w in enumerate(range(*quads[q])):
                t2[q] = pe.did(nc.tensor.transpose(bank[4 + q % 2][0:D, j * P:(j + 1) * P], hr[:, w, 0:D], ident[:, :]))

        def copy_h(q):
            n = (quads[q][1] - quads[q][0]) * P
            ac.wait(t2[q], *([ab[q - 2]] if q >= 2 else []))
            c2[q] = ac.did(nc.scalar.copy(feat[q % 2][0:D, 0:n], bank[4 + q % 2][0:D, 0:n]))

        def project(q):
            pe.wait(c2[q], ones_row, edge_here, *([cp[q - 2], r1[q - 2]] if q >= 2 else []))
            for j in range(quads[q][1] - quads[q][0]):
                ab[q] = pe.did(nc.tensor.matmul(bank[6 + q % 2][:, j * P:(j + 1) * P], feat[q % 2][:, j * P:(j + 1) * P],
                                                wedge[:, :], start=True, stop=True))

        def split(q):
            a, b = quads[q]
            both = bank[6 + q % 2][:, 0:(b - a) * P].rearrange("p (w c) -> p w c", c=P)
            part = [b_part[:, a:b, k * D:(k + 1) * D] for k in range(3)]
            r, s = rest[q % 2][:, 0:b - a, :], rest2[q % 2][:, 0:b - a, :]
            ac.wait(ab[q], *([st[q - 4]] if q >= 4 else []))
            b1[q] = ac.did(nc.scalar.copy(part[0], both[:, :, D:2 * D]))
            cp[q] = ac.did(nc.scalar.copy(a_out[q % 4][:, 0:b - a, :], both[:, :, 0:D]))
            ve.wait(cp[q])
            r1[q] = ve.did(nc.vector.tensor_tensor(r, both[:, :, D:2 * D], part[0], ALU.subtract))
            ve.wait(r1[q])
            done = ve.did(nc.vector.tensor_copy(part[1], r))
            ve.wait(done)
            b3[q] = ve.did(nc.vector.tensor_tensor(part[2], r, part[1], ALU.subtract))
            st[q] = store(table, q % 4, (a, b), a_out[q % 4][:, 0:b - a, :], cp[q])

        stages = ([turn_both, copy_both, update, activate] if node_here else []) + \
            ([turn_h, copy_h, project, split] if edge_here else [])
        staged(len(quads), stages)
        last = len(quads) - 1
        return [b3[last], cp[last], (pe.sem, pe.count)] + [(s_t[n], stores[n]) for n in range(4)] if edge_here else [h1[last]]

    s_t += [sem(f"s_table{n}") for n in (2, 3)]
    stores += [0, 0]

    xt_free = (pe.sem, pe.count)
    for lane in (ve, po, ac):
        lane.wait(xt_free)
    start_points = table_here + [pt["bank7"], (s_pw, 16), (pe.sem, pe.count), (ve.sem, ve.count)]
    edge_pass(0, tables[0], start_points, False)
    for w in wtraj:
        wt_zero = ve.did(nc.vector.memset(w[:, :], 0.0))
    nc.sync.wait_ge(*wt_zero)
    edge_here = load_layer(0, None)
    for c in range(NW // ROWS):
        normed = attention_out(c)
    ready = dense(None, edge_here, lambda q: normed, tables[1])
    for layer in range(LAYERS):
        edge_pass(1 + layer, tables[(layer + 1) % 2], ready, True)
        node_here = load_node(layer)
        more = layer + 1 < LAYERS
        edge_here = load_layer(layer + 1, None) if more else None
        node_here = (s_lw, lw[0])
        for c in range(NW // ROWS):
            a, b = c * ROWS, (c + 1) * ROWS
            summed = ve.did(nc.vector.tensor_tensor(hr[:, a:b, D:2 * D], hr[:, a:b, D:2 * D], red1[:, a:b, :], ALU.add))
        ready = dense(node_here, edge_here, lambda q: summed, tables[layer % 2])

    s_out = sem("s_out")
    ve.wait(*ready)
    for c in range(NW // ROWS):
        a, b = c * ROWS, (c + 1) * ROWS
        tmp = work[:, 1024:1024 + ROWS * D].rearrange("p (w d) -> p w d", d=D)
        value = hr[:, a:b, 0:D]
        done = ve.did(nc.vector.tensor_tensor(value, value, x1[:, a:b, :], ALU.add))
        ve.wait(done)
        done = normalise(value, ROWS, red1[:, a:b, :], work[:, 2048:2048 + 2 * ROWS], tmp)
        nc.sync.wait_ge(*done)
        whole = min(b, NW - 1)
        nc.sync.dma_start(out[a * P:whole * P, :].rearrange("(w p) d -> p w d", p=P), red1[:, a:whole, :]).then_inc(s_out, 16)
    nc.sync.dma_start(out[full:N, :], red1[0:TAIL, NW - 1, :]).then_inc(s_out, 16)
    nc.sync.wait_ge(s_out, 16 * (NW // ROWS + 1))
    ctx.close()


def kernel(**inputs):
    import concourse.bacc as bacc
    from concourse.bass_utils import run_bass_kernel_spmd

    get = lambda n: np.asarray(inputs[n])
    arrays = {n: np.ascontiguousarray(get(n)) for n in ("x", "src", "dst", "edge_weight")}
    arrays["w_head"] = np.ascontiguousarray(get("L0_gnn_Wh").transpose(1, 0, 2).reshape(D, H * D))
    arrays["w_out"] = np.ascontiguousarray(get("L0_gnn_weight").reshape(H, D, D).transpose(1, 0, 2).reshape(D, H * D))
    edge, node = ([get(f"L1_gnn_{k}{n}") for n in range(LAYERS)] for k in ("We", "Wn"))
    be, bn = ([get(f"L1_gnn_{k}{n}") for n in range(LAYERS)] for k in ("be", "bn"))
    arrays["w_edge"] = np.stack([np.concatenate([w[:, :D].T, w[:, D:2 * D].T], axis=1) for w in edge])
    arrays["b_edge"] = np.stack([np.concatenate([np.zeros_like(b), b])[None] for b in be])
    arrays["w_traj"] = np.stack([w[:, 2 * D][None] for w in edge])
    arrays["w_node"] = np.stack([w.T for w in node])
    arrays["b_node"] = np.stack([b[None] for b in bn])
    nc = bacc.Bacc("TRN2", target_bir_lowering=False, num_devices=1)
    feed, args = {}, []
    for name, a in arrays.items():
        a = np.ascontiguousarray(a)
        feed[f"in_{name}"] = a
        args.append(nc.dram_tensor(f"in_{name}", a.shape, mybir.dt.from_np(a.dtype), kind="ExternalInput").ap())
    args.append(nc.dram_tensor("out_0", (N, D), F32, kind="ExternalOutput").ap())
    build(nc, *args)
    r = run_bass_kernel_spmd(nc, [feed], core_ids=[0])
    return r.results[0]["out_0"]
```
